# Optimizing a Trainium2 kernel written in Bass

```python
import numpy as np
import jax
import jax.numpy as jnp

def _softmax(x, axis=-1):
    return jax.nn.softmax(x, axis=axis)

def _gelu(x):
    return jax.nn.gelu(x, approximate=True)

def _silu(x):
    return jax.nn.silu(x)

def _sigmoid(x):
    return jax.nn.sigmoid(x)

def _layernorm(x, axis=-1, eps=1e-05):
    m = jnp.mean(x, axis=axis, keepdims=True)
    v = jnp.var(x, axis=axis, keepdims=True)
    return (x - m) / jnp.sqrt(v + eps)

def _scatter_add(tgt, idx, src, axis=0):
    return tgt.at[idx].add(src)

def _segment_sum(src, seg, n):
    return jax.ops.segment_sum(src, seg, n)
kernel_name = 'mk_gnn_preln_d2_gnn_r8_7b115a'

def setup_inputs(seed: int=0):
    np.random.seed(seed)
    _w = jnp.asarray

    def _rec_inputs():
        import jax
        import jax.numpy as jnp
        _gk = jax.random.key(seed)
        x = -0.0003713 + 1 * jax.random.normal(jax.random.fold_in(_gk, 1), (12500, 128), jnp.float32)
        _s = jax.random.randint(jax.random.fold_in(_gk, 2), (100000,), 0, 12500, jnp.int32)
        _d = jax.random.randint(jax.random.fold_in(_gk, 3), (100000,), 0, 12500, jnp.int32)
        _loop = jnp.arange(12500, dtype=jnp.int32)
        src = jnp.concatenate([_s, _d, _loop])
        dst = jnp.concatenate([_d, _s, _loop])
        _o = jnp.argsort(dst, stable=True)
        src = src[_o]
        dst = dst[_o]
        edge_type_8 = jax.random.randint(jax.random.fold_in(_gk, 13), (212500,), 0, 8, jnp.int32)
        return (x, src, dst, edge_type_8)
    x, src, dst, edge_type_8 = _rec_inputs()

    def _L0_gnn_setup():
        import jax, jax.numpy as jnp
        import numpy as np
        N, E, D, R, H = (12500, 75000, 128, 8, 512)

        def _layernorm(x, g, b, eps=1e-05):
            mu = jnp.mean(x, axis=-1, keepdims=True)
            var = jnp.mean((x - mu) ** 2, axis=-1, keepdims=True)
            return (x - mu) / jnp.sqrt(var + eps) * g + b
        key = jax.random.key(seed)
        ks = jax.random.split(key, 9)
        s = 0.02
        return {'x': jax.random.normal(ks[0], (N, D), dtype=jnp.float32), 'src': jax.random.randint(ks[1], (E,), 0, N, dtype=jnp.int32), 'dst': jax.random.randint(ks[2], (E,), 0, N, dtype=jnp.int32), 'edge_type': jax.random.randint(ks[3], (E,), 0, R, dtype=jnp.int32), 'W_rel': jax.random.normal(ks[4], (R, D, D), dtype=jnp.float32) * s, 'W_self': jax.random.normal(ks[5], (D, D), dtype=jnp.float32) * s, 'b_conv': jnp.zeros((D,), dtype=jnp.float32), 'ln1_g': jnp.ones((D,), dtype=jnp.float32), 'ln1_b': jnp.zeros((D,), dtype=jnp.float32), 'ln2_g': jnp.ones((D,), dtype=jnp.float32), 'ln2_b': jnp.zeros((D,), dtype=jnp.float32), 'W1': jax.random.normal(ks[6], (D, H), dtype=jnp.float32) * s, 'b1': jnp.zeros((H,), dtype=jnp.float32), 'W2': jax.random.normal(ks[7], (H, D), dtype=jnp.float32) * s, 'b2': jnp.zeros((D,), dtype=jnp.float32)}
    _L0_gnn_all = _L0_gnn_setup()
    _L0_gnn_in = {k: v for k, v in _L0_gnn_all.items() if k in ('W_rel', 'W_self', 'b_conv', 'ln1_g', 'ln1_b', 'ln2_g', 'ln2_b', 'W1', 'b1', 'W2', 'b2')}
    del _L0_gnn_all

    def _L1_gnn_setup():
        import jax, jax.numpy as jnp
        import numpy as np
        N = 6250
        E = 75000
        IN = 128
        H = 4
        C = 32
        B = 3
        NEG_SLOPE = 0.2
        key = jax.random.key(seed)
        ks = jax.random.split(key, 6)
        x = jax.random.normal(ks[0], (N, IN), dtype=jnp.float32)
        edge_index = jax.random.randint(ks[1], (2, E), 0, N)
        coeffs_t = jnp.array([0.25, 0.5, 0.25], dtype=jnp.float32)
        glorot_w = float(np.sqrt(2.0) * np.sqrt(6.0 / (H * C + IN)))
        glorot_a = float(np.sqrt(2.0) * np.sqrt(6.0 / (1 + C)))
        lin_weight = jax.random.uniform(ks[2], (B, H * C, IN), jnp.float32, -glorot_w, glorot_w)
        lin_bias = jnp.zeros((B, H * C), dtype=jnp.float32)
        att_src = jax.random.uniform(ks[3], (B, 1, H, C), jnp.float32, -glorot_a, glorot_a)
        att_dst = jax.random.uniform(ks[4], (B, 1, H, C), jnp.float32, -glorot_a, glorot_a)
        return {'x': x, 'edge_index': edge_index, 'coeffs_t': coeffs_t, 'lin_weight': lin_weight, 'lin_bias': lin_bias, 'att_src': att_src, 'att_dst': att_dst}
    _L1_gnn_all = _L1_gnn_setup()
    _L1_gnn_in = {k: v for k, v in _L1_gnn_all.items() if k in ('coeffs_t', 'lin_weight', 'lin_bias', 'att_src', 'att_dst')}
    del _L1_gnn_all
    return {'x': x, 'src': src, 'dst': dst, 'edge_type_8': edge_type_8, 'L0_gnn_W_rel': _L0_gnn_in['W_rel'], 'L0_gnn_W_self': _L0_gnn_in['W_self'], 'L0_gnn_b_conv': _L0_gnn_in['b_conv'], 'L0_gnn_ln1_g': _L0_gnn_in['ln1_g'], 'L0_gnn_ln1_b': _L0_gnn_in['ln1_b'], 'L0_gnn_ln2_g': _L0_gnn_in['ln2_g'], 'L0_gnn_ln2_b': _L0_gnn_in['ln2_b'], 'L0_gnn_W1': _L0_gnn_in['W1'], 'L0_gnn_b1': _L0_gnn_in['b1'], 'L0_gnn_W2': _L0_gnn_in['W2'], 'L0_gnn_b2': _L0_gnn_in['b2'], 'L1_gnn_coeffs_t': _L1_gnn_in['coeffs_t'], 'L1_gnn_lin_weight': _L1_gnn_in['lin_weight'], 'L1_gnn_lin_bias': _L1_gnn_in['lin_bias'], 'L1_gnn_att_src': _L1_gnn_in['att_src'], 'L1_gnn_att_dst': _L1_gnn_in['att_dst']}

def reference(x, src, dst, edge_type_8, L0_gnn_W_rel, L0_gnn_W_self, L0_gnn_b_conv, L0_gnn_ln1_g, L0_gnn_ln1_b, L0_gnn_ln2_g, L0_gnn_ln2_b, L0_gnn_W1, L0_gnn_b1, L0_gnn_W2, L0_gnn_b2, L1_gnn_coeffs_t, L1_gnn_lin_weight, L1_gnn_lin_bias, L1_gnn_att_src, L1_gnn_att_dst):
    import jax
    import jax.numpy as jnp

    def _L0_gnn_ref(x, src, dst, edge_type, W_rel, W_self, b_conv, ln1_g, ln1_b, ln2_g, ln2_b, W1, b1, W2, b2):
        import jax, jax.numpy as jnp
        import numpy as np
        N, E, D, R, H = (12500, 75000, 128, 8, 512)

        def _layernorm(x, g, b, eps=1e-05):
            mu = jnp.mean(x, axis=-1, keepdims=True)
            var = jnp.mean((x - mu) ** 2, axis=-1, keepdims=True)
            return (x - mu) / jnp.sqrt(var + eps) * g + b
        n = x.shape[0]
        xW = jnp.einsum('nd,rde->nre', x, W_rel)
        msg = xW[src, edge_type]
        agg = jax.ops.segment_sum(msg, dst, num_segments=n)
        h = agg + x @ W_self + b_conv
        h = jax.nn.gelu(_layernorm(h, ln1_g, ln1_b), approximate=False)
        x = x + h
        ff = _layernorm(x, ln2_g, ln2_b)
        ff = jax.nn.gelu(ff @ W1 + b1, approximate=False) @ W2 + b2
        return x + ff

    def _L1_gnn_ref(x, edge_index, coeffs_t, lin_weight, lin_bias, att_src, att_dst):
        import jax, jax.numpy as jnp
        import numpy as np
        N = 6250
        E = 75000
        IN = 128
        H = 4
        C = 32
        B = 3
        NEG_SLOPE = 0.2
        W = jnp.einsum('b,boi->oi', coeffs_t, lin_weight)
        bias = jnp.einsum('b,bo->o', coeffs_t, lin_bias)
        a_src = jnp.einsum('b,bqhc->qhc', coeffs_t, att_src)
        a_dst = jnp.einsum('b,bqhc->qhc', coeffs_t, att_dst)
        n = x.shape[0]
        xt = (x @ W.T + bias).reshape(n, H, C)
        alpha_src = jnp.sum(xt * a_src, axis=-1)
        alpha_dst = jnp.sum(xt * a_dst, axis=-1)
        row, col = (edge_index[0], edge_index[1])
        alpha = alpha_src[row] + alpha_dst[col]
        alpha = jax.nn.leaky_relu(alpha, NEG_SLOPE)
        amax = jax.ops.segment_max(alpha, col, num_segments=n)
        ex = jnp.exp(alpha - amax[col])
        denom = jax.ops.segment_sum(ex, col, num_segments=n)
        alpha = ex / (denom[col] + 1e-16)
        msg = xt[row] * alpha[..., None]
        out = jax.ops.segment_sum(msg, col, num_segments=n)
        return out.reshape(n, H * C)
    edge_index = jnp.stack([src, dst])
    h = jnp.maximum(_layernorm(x, axis=-1), 0.0)
    x = x + _L0_gnn_ref(h, src, dst, edge_type_8, L0_gnn_W_rel, L0_gnn_W_self, L0_gnn_b_conv, L0_gnn_ln1_g, L0_gnn_ln1_b, L0_gnn_ln2_g, L0_gnn_ln2_b, L0_gnn_W1, L0_gnn_b1, L0_gnn_W2, L0_gnn_b2)
    h = jnp.maximum(_layernorm(x, axis=-1), 0.0)
    x = x + _L1_gnn_ref(h, edge_index, L1_gnn_coeffs_t, L1_gnn_lin_weight, L1_gnn_lin_bias, L1_gnn_att_src, L1_gnn_att_dst)
    return x

_drawn_inputs = setup_inputs


def setup_inputs(seed=0):
    import zlib

    import numpy as np

    out = dict(_drawn_inputs(seed))
    spreads = {'L0_gnn_b_conv': (0.0, 0.1),
     'L0_gnn_ln1_g': (1.0, 0.2),
     'L0_gnn_ln1_b': (0.0, 0.1),
     'L0_gnn_ln2_g': (1.0, 0.6),
     'L0_gnn_ln2_b': (0.0, 0.8),
     'L0_gnn_b1': (0.0, 0.569),
     'L0_gnn_b2': (0.0, 0.1),
     'L1_gnn_lin_bias': (0.0, 0.1)}
    factors = {'L1_gnn_att_dst': 11.777}
    for name, (base, spread) in spreads.items():
        noise = np.random.default_rng([zlib.crc32(name.encode()), seed]).standard_normal(out[name].shape)
        drawn = base * np.exp(spread * noise) if base else spread * noise
        out[name] = jnp.asarray(drawn.astype(out[name].dtype))
    for name, factor in factors.items():
        out[name] = (out[name] * factor).astype(out[name].dtype)
    return out
```

```python
import concourse.bass as bass
import numpy as np
from concourse import mybir
from contextlib import ExitStack

P = 128
N, E, D, R, H = 12500, 212500, 128, 8, 512
HEADS, HC = 4, 32
BLOCKS = -(-N // P)
TAIL_ROWS = N - (BLOCKS - 1) * P
CHUNKS = 16
GROUP = CHUNKS * P
GROUPS = -(-E // GROUP)
LAST_FULL = (E - (GROUPS - 1) * GROUP) // CHUNKS
LAST_REST = (E - (GROUPS - 1) * GROUP) % CHUNKS
PAD_ROWS = (BLOCKS + 1) * P
BATCH = 7
BATCHES = BLOCKS // BATCH
XT = D + HEADS
ST = D + 2 * HEADS
BIG = float(2.0 ** 100)
EPS = 1e-5
MAGIC = float(0x5F3759DF)
NEWTON = 3
assert BLOCKS % BATCH == 0 and GROUPS % 2 == 0 and BLOCKS % 2 == 0

f32, bf16 = mybir.dt.float32, mybir.dt.bfloat16
i32, u32 = mybir.dt.int32, mybir.dt.uint32
ALU = mybir.AluOpType
ACT = mybir.ActivationFunctionType
AX = mybir.AxisListType


class Chain:

    def __init__(self, eng, sem, base=0):
        self.eng, self.sem, self.base, self.n = eng, sem, base, 0

    def step(self, ins):
        self.n += 1
        ins.then_inc(self.sem, 1)
        self.eng.wait_ge(self.sem, self.base + self.n)


class Stops:

    def __init__(self, sem):
        self.sem = sem

    def __call__(self, eng):
        eng.sem_inc(self.sem, 1)


RSQRT_STEPS = 3 + 4 * NEWTON


def rsqrt_steps(nc, chain, out, var, tmp):
    v = nc.vector
    chain.step(v.tensor_scalar(tmp, var, EPS, None, ALU.add))
    chain.step(v.tensor_scalar(out.bitcast(i32), tmp.bitcast(i32), 1, None, ALU.arith_shift_right))
    chain.step(v.tensor_scalar(out.bitcast(i32), out.bitcast(i32), -1.0, MAGIC, ALU.mult, ALU.add))
    for _ in range(NEWTON):
        sq = var
        chain.step(v.tensor_tensor(sq, out, out, ALU.mult))
        chain.step(v.tensor_tensor(sq, sq, tmp, ALU.mult))
        chain.step(v.tensor_scalar(sq, sq, -0.5, 1.5, ALU.mult, ALU.add))
        chain.step(v.tensor_tensor(out, out, sq, ALU.mult))


STATS_STEPS = 2 + RSQRT_STEPS + 2


def stats_steps(nc, chain, stop, rows, stats, mv, mean, var, tmp, rstd, shift):
    v = nc.vector
    n = len(rows)
    stop(chain.eng)
    for j, row in enumerate(rows[:-1]):
        v.bn_stats(stats[:, j, :], row)
    chain.step(v.bn_stats(stats[:, n - 1, :], rows[-1]))
    stop(chain.eng)
    for j in range(n - 1):
        v.bn_aggr(mv[:, j, :], stats[:, j, :])
    chain.step(v.bn_aggr(mv[:, n - 1, :], stats[:, n - 1, :]))
    chain.step(v.tensor_copy(var, mv[:, :, 1]))
    rsqrt_steps(nc, chain, rstd, var, tmp)
    chain.step(v.scalar_tensor_tensor(shift, mv[:, :, 0], -1.0, rstd, ALU.mult, ALU.mult))


def build(nc, x, src, dst, typ, W_rel, W_self, b_conv, g1, b1n, g2, b2n, W1, b1, W2, b2,
          coeffs, lin_w, lin_b, att_src, att_dst, out):
    dram = lambda name, shape, dt=f32: nc.dram_tensor(name, shape, dt).ap()
    rel_table = dram("rel_table", (BLOCKS * P * R, D))
    agg_state = dram("agg_state", (PAD_ROWS, D))
    xt_table = dram("xt_table", (PAD_ROWS, XT))
    ad_table = dram("ad_table", (PAD_ROWS, HEADS))
    att_state = dram("att_state", (PAD_ROWS, ST))

    ctx = ExitStack()
    with ctx:
        sb = lambda name, shape, dt=f32: ctx.enter_context(nc.sbuf_tensor(name, shape, dt))
        pb = lambda name, shape, dt=f32: ctx.enter_context(nc.psum_tensor(name, shape, dt))
        sem = lambda name: ctx.enter_context(nc.semaphore(name))

        ident = sb("ident", [P, P])
        ident4 = sb("ident4", [P, HEADS, P], bf16)
        iota = sb("iota", [P, P])
        pick = sb("pick", [96, 32], bf16)
        upper = sb("upper", [P, P])
        zeros = sb("zeros", [P, ST])
        w_all = sb("w_all", [P, R * D + D])
        w1 = sb("w1", [P, H])
        w2 = sb("w2", [P, H // P, D])
        b1col = sb("b1col", [P, H // P])
        wx = sb("wx", [P, XT + HEADS])
        bx = sb("bx", [P, XT + HEADS])
        rows = sb("rows", [P, 4, D])
        cols = sb("cols", [P, 2])
        linw = sb("linw", [P, 3, D])
        linb = sb("linb", [P, 3])
        atts = sb("atts", [P, 2, 3])
        coef = sb("coef", [P, 3])
        wcomb = sb("wcomb", [P, D])
        acomb = sb("acomb", [P, 2])
        bcomb = sb("bcomb", [P, 1])
        a8 = sb("a8", [P, D + 2 * HEADS])

        x_res = sb("x_res", [P, BLOCKS + 2, D])
        h_res = sb("h_res", [P, BLOCKS, D])
        src_all = sb("src_all", [P, GROUPS + 2, CHUNKS], i32)
        idx0_all = sb("idx0_all", [P, GROUPS + 2, CHUNKS], i32)
        dst_raw = sb("dst_raw", [P, GROUPS, CHUNKS], i32)
        dst_all = sb("dst_all", [P, GROUPS, CHUNKS])
        span = sb("span", [P, 2, GROUPS])
        spanc = sb("spanc", [GROUPS, 4])
        spani = sb("spani", [GROUPS, 1], i32)
        base_all = sb("base_all", [P, GROUPS])
        plan = sb("plan", [1, GROUPS, 4], i32)

        stats = sb("stats", [P, BATCH, 6])
        mv = sb("mv", [P, BATCH, 2])
        var = sb("var", [P, BATCH])
        tmp = sb("tmp", [P, BATCH])
        rstd = sb("rstd", [P, BATCH])
        shift = sb("shift", [P, BATCH])
        rstd_all = sb("rstd_all", [P, BLOCKS + 2])
        shift_all = sb("shift_all", [P, BLOCKS + 2])
        hs = sb("hs", [P, 2, D])
        hT = sb("hT", [P, 2, D])
        xw = sb("xw", [P, 2, R * D + D])

        idx = sb("idx", [P, 2, CHUNKS], u32)
        rel = sb("rel", [P, CHUNKS])
        G = sb("G", [P, 2, CHUNKS, XT])
        onehot = sb("onehot", [P, CHUNKS, P])
        old = sb("old", [P, ST])
        new = sb("new", [P, ST])

        A = sb("A", [P, BATCH, D])
        B = sb("B", [P, BATCH, D])

        pairs = [pb(f"pair{i}", [P, 1024]) for i in range(2)]
        banks = [pairs[i // 2][:, (i % 2) * 512:(i % 2) * 512 + 512] for i in range(4)] + \
                [pb(f"bank{i}", [P, 512])[:, :] for i in range(4, 8)]
        score = [pr[:, :].rearrange("p (c h e) -> p c h e", c=2, h=HEADS) for pr in pairs]

        s_const, s_pool, s_load, s_x, s_edges = (sem(n) for n in ("s_const", "s_pool", "s_load", "s_x", "s_edges"))
        s_edges_set, s_set, s_setpe, s_setdve, s_plan = (sem(n) for n in ("s_edges_set", "s_set", "s_setpe", "s_setdve", "s_plan"))
        c_dve = sem("c_dve")
        h_norm, h_ready, h_saved, hT_ps, hT_sb, xw_ps, xwA_sb, xwB_sb = (sem(n) for n in (
            "h_norm", "h_ready", "h_saved", "hT_ps", "hT_sb", "xw_ps", "xwA_sb", "xwB_sb"))
        s_store = [sem("s_store0"), sem("s_store1")]
        s_agg = sem("s_agg")
        ff_ready, split_chain = sem("ff_ready"), sem("split_chain")

        def edge_sems(k):
            n = dict(idx_ready=sem(f"idx_ready{k}"), gathered=[sem(f"gathered{k}_{i}") for i in range(2)],
                     group_free=sem(f"group_free{k}"), oh_ready=sem(f"oh_ready{k}"), agg_done=sem(f"agg_done{k}"),
                     merged=sem(f"merged{k}"), old_ready=sem(f"old_ready{k}"), chain=sem(f"chain{k}"))
            return n

        e0, e1 = edge_sems(0), edge_sems(1)
        att_stored = sem("att_stored")
        tables_ready = [sem("tables_ready0"), sem("tables_ready1")]

        c_dense = sem("c_dense")
        a_load, n1_ready, g_in, g_out, n2_ready, x2_ready, t_ps, t_sb, up_ps, up_sb, down_ps, x1_ready, h1_ready, xt_ps, xt_sb = (
            sem(n) for n in ("a_load", "n1_ready", "g_in", "g_out", "n2_ready", "x2_ready", "t_ps", "t_sb", "up_ps",
                             "up_sb", "down_ps", "x1_ready", "h1_ready", "xt_ps", "xt_sb"))
        s_xt = sem("s_xt")

        ad_ready, mask_ready, parts_ready, partsT_ps, partsT_sb, ohT_ps, ohT_sb, score_ps, score_used = (
            sem(n) for n in ("ad_ready", "mask_ready", "parts_ready", "partsT_ps", "partsT_sb", "ohT_ps", "ohT_sb",
                             "score_ps", "score_used"))
        c_ready, c_ps, arg_ready, w_ready, msg_ready, marg_ready, mexp_ready = (
            sem(n) for n in ("c_ready", "c_ps", "arg_ready", "w_ready", "msg_ready", "marg_ready", "mexp_ready"))
        fin_load, fin_done, s_out = [sem("fin_load0"), sem("fin_load1")], sem("fin_done"), [sem("s_out0"), sem("s_out1")]
        c_fin, merge_chain = sem("c_fin"), sem("merge_chain")

        mask = sb("mask", [P, CHUNKS, P], bf16)
        ohT = sb("ohT", [P, CHUNKS, P], bf16)
        parts = sb("parts", [P, 2, 3, 32], bf16)
        resid = sb("resid", [P, 2, 32])
        partsT = sb("partsT", [96, 2, P], bf16)
        adw = sb("adw", [P, HEADS])
        mk = sb("mk", [P, CHUNKS, HEADS])
        mg = sb("mg", [P, HEADS])
        iotab = sb("iotab", [P, P], bf16)
        cparts = sb("cparts", [P, 3, 2 * HEADS], bf16)
        cres = sb("cres", [P, 2 * HEADS])
        cbs = sb("cbs", [P, CHUNKS, 2 * HEADS])
        ca = sb("ca", [P, 2 * HEADS])
        z = sb("z", [P, CHUNKS, HEADS])
        z2 = sb("z2", [P, CHUNKS, HEADS])
        h_flat = h_res[:, :, :].rearrange("p b d -> p (b d)")
        M = h_flat[:, 0:CHUNKS * XT].rearrange("p (c k) -> p c k", c=CHUNKS)
        cc = sb("cc", [P, 6, HEADS])
        marg = sb("marg", [P, 2 * HEADS])
        mexp = sb("mexp", [P, 2 * HEADS])
        scaled = sb("scaled", [P, XT])

        tT = sb("tT", [P, 2, P])
        hid = onehot[:, :, :].rearrange("p a b -> p (a b)")[:, 0:2 * H].rearrange("p (s c n) -> p s c n", s=2, c=H // P)
        xt_sbuf = G[:, 0, :, :].rearrange("p a b -> p (a b)")[:, 0:2 * (XT + HEADS)].rearrange("p (s n) -> p s n", s=2)
        fin = G[:, :, 0:BATCH, :].rearrange("p s b d -> p s (b d)")

        dve_stop, pe_stop, sp_stop, pool_stop = (Stops(sem(f"{n}_stop")) for n in ("dve", "pe", "sp", "pool"))

        def load_plan(eng, g):
            base = eng.value_load(plan[0:1, bass.ds(g, 1), 0:1], min_val=0, max_val=N - 1)
            windows = eng.value_load(plan[0:1, bass.ds(g, 1), 1:2], min_val=1, max_val=BLOCKS)
            passes = eng.value_load(plan[0:1, bass.ds(g, 1), 2:3], min_val=0, max_val=GROUPS * BLOCKS)
            return base, windows, passes

        block = ctx.enter_context(nc.Block())

        def store_out(sp, q):
            s = q % 2
            sp.wait_ge(fin_done, q + 1)
            lo = q * BATCH
            nb = BATCH - 1 if q == BATCHES - 1 else BATCH
            sp.dma_start(out[lo * P:(lo + nb) * P, :].rearrange("(b p) d -> p b d", p=P),
                         x_res[:, lo:lo + nb, :]).then_inc(s_out[s], 16)
            if q == BATCHES - 1:
                sp.dma_start(out[(BLOCKS - 1) * P:N, :], x_res[0:TAIL_ROWS, BLOCKS - 1, :]).then_inc(s_out[s], 16)

        @block.sync
        def _(sp):
            full = E - (E - (GROUPS - 1) * GROUP)
            sp.wait_ge(s_edges_set, 3)
            for tile, arr in ((src_all, src), (idx0_all, typ), (dst_raw, dst)):
                sp.dma_start(tile[:, 0:GROUPS - 1, :],
                             arr[0:full].rearrange("(g p c) -> p g c", p=P, c=CHUNKS)).then_inc(s_edges, 16)
                sp.dma_start(tile[0:LAST_FULL, GROUPS - 1, :],
                             arr[full:full + LAST_FULL * CHUNKS].rearrange("(p c) -> p c", c=CHUNKS)).then_inc(s_edges, 16)
                sp.dma_start(tile[LAST_FULL:LAST_FULL + 1, GROUPS - 1, 0:LAST_REST],
                             arr[full + LAST_FULL * CHUNKS:E].rearrange("(p c) -> p c", p=1)).then_inc(s_edges, 16)
            sp.wait_ge(s_pool, 9)
            sp.dma_start(agg_state[BLOCKS * P:PAD_ROWS, :], zeros[:, 0:D]).then_inc(s_agg, 16)
            sp.dma_start(ad_table[BLOCKS * P:PAD_ROWS, :], zeros[:, 0:HEADS]).then_inc(s_store[0], 16)
            sp.dma_start(xt_table[BLOCKS * P:PAD_ROWS, :], zeros[:, 0:XT]).then_inc(s_store[1], 16)
            sp.dma_start(att_state.rearrange("(b p) c -> p b c", p=P),
                         zeros[:, :].rearrange("p (o c) -> p o c", o=1).to_broadcast([P, BLOCKS + 1, ST])).then_inc(att_stored, 16)

            with sp.Fori(0, BLOCKS // 2) as i:
                for s in range(2):
                    b = i * 2 + s
                    sp.wait_ge(xwA_sb, b + 3)
                    sp.wait_ge(xwB_sb, b + 3)
                    sp.dma_start(rel_table.rearrange("(n r) e -> n (r e)", r=R)[bass.ds(b * P, P), :],
                                 xw[:, s, 0:R * D]).then_inc(s_store[s], 16)
                    sp.dma_start(agg_state[bass.ds(b * P, P), :], xw[:, s, R * D:]).then_inc(s_store[s], 16)
            for s in range(2):
                sp.wait_ge(s_store[s], 16 + 32 * (BLOCKS // 2))
            sp.sem_inc(tables_ready[0], 1)

            with sp.Fori(0, GROUPS) as g:
                base, windows, passes = load_plan(sp, g)
                with sp.Fori(0, windows) as w:
                    t = passes + w
                    row = nc.s_assert_within(base + w * P, 0, N - 1, skip_runtime_bounds_check_because="it is at most the group's greatest destination")
                    sp.wait_ge(s_agg, (t + 1) * 16)
                    sp.dma_start(old[:, 0:D], agg_state[bass.ds(row, P), :]).then_inc(e0["old_ready"], 16)
                    sp.wait_ge(e0["merged"], t + 2)
                    sp.dma_start(agg_state[bass.ds(row, P), :], new[:, 0:D]).then_inc(s_agg, 16)
            total = sp.value_load(plan[0:1, 0:1, 3:4], min_val=1, max_val=GROUPS * BLOCKS)
            sp.wait_ge(s_agg, (total + 1) * 16)
            sp_stop(sp)

            with sp.Fori(0, BATCHES) as q:
                sp.wait_ge(x2_ready, q + 1)
                sp.dma_start(A[:, :, :], agg_state[bass.ds(q * (BATCH * P), BATCH * P), :].rearrange("(b p) d -> p b d", p=P)).then_inc(a_load, 16)
                with sp.Fori(0, BATCH) as j:
                    b = q * BATCH + j
                    sp.wait_ge(xt_sb, b + 1)
                    sp.dma_start(xt_table[bass.ds(b * P, P), :], xt_sbuf[:, 0, 0:XT]).then_inc(s_xt, 16)
                    sp.dma_start(ad_table[bass.ds(b * P, P), :], xt_sbuf[:, 0, XT:]).then_inc(s_xt, 16)
            sp.wait_ge(s_xt, 32 * BLOCKS)
            sp.sem_inc(tables_ready[1], 1)

            with sp.Fori(0, GROUPS) as g:
                base, windows, passes = load_plan(sp, g)
                with sp.Fori(0, windows) as w:
                    t = passes + w
                    row = nc.s_assert_within(base + w * P, 0, N - 1, skip_runtime_bounds_check_because="it is at most the group's greatest destination")
                    sp.wait_ge(e1["merged"], t + 1)
                    sp.dma_start(adw[:, :], ad_table[bass.ds(row, P), :]).then_inc(ad_ready, 16)
                    sp.wait_ge(att_stored, (t + 1) * 16)
                    sp.dma_start(old[:, :], att_state[bass.ds(row, P), :]).then_inc(e1["old_ready"], 16)
                    sp.wait_ge(e1["merged"], t + 2)
                    sp.dma_start(att_state[bass.ds(row, P), :], new[:, :]).then_inc(att_stored, 16)
            total = sp.value_load(plan[0:1, 0:1, 3:4], min_val=1, max_val=GROUPS * BLOCKS)
            sp.wait_ge(att_stored, (total + 1) * 16)

            for q in range(BATCHES):
                s = q % 2
                if q >= 2:
                    sp.wait_ge(s_out[s], 16 * (q // 2))
                sp.dma_start(fin[:, s, 0:BATCH * XT].rearrange("p (b c) -> p b c", c=XT),
                             att_state[q * BATCH * P:(q + 1) * BATCH * P, 0:XT].rearrange("(b p) c -> p b c", p=P)).then_inc(fin_load[s], 16)
                if q >= 1:
                    store_out(sp, q - 1)
            store_out(sp, BATCHES - 1)
            for s in range(2):
                n = len([q for q in range(BATCHES) if q % 2 == s])
                sp.wait_ge(s_out[s], 16 * n + (16 if s == (BATCHES - 1) % 2 else 0))

        @block.gpsimd
        def _(pool):
            g = nc.gpsimd
            g.memset(x_res[:, BLOCKS - 1:, :], 0.0).then_inc(s_const, 1)
            g.memset(rstd_all[:, :], 0.0).then_inc(s_const, 1)
            g.memset(shift_all[:, :], 0.0).then_inc(s_const, 1)
            g.memset(src_all[:, GROUPS - 1:, :], 0).then_inc(s_edges_set, 1)
            g.memset(idx0_all[:, GROUPS - 1:, :], 0).then_inc(s_edges_set, 1)
            g.memset(dst_raw[:, GROUPS - 1:, :], -1).then_inc(s_edges_set, 1)
            g.memset(ident[:, :], 0.0).then_inc(s_pool, 1)
            g.memset(ident4[:, :, :], 0.0).then_inc(s_pool, 1)
            g.memset(pick[:, :], 0.0).then_inc(s_pool, 1)
            g.memset(upper[:, :], 1.0).then_inc(s_pool, 1)
            g.memset(a8[:, D:], 0.0).then_inc(s_pool, 1)
            g.memset(parts[:, :, :, :], 0.0).then_inc(s_pool, 1)
            g.memset(zeros[:, 0:XT], 0.0).then_inc(s_pool, 1)
            g.memset(zeros[:, XT:], -BIG).then_inc(s_pool, 1)
            g.iota(iota[:, :], pattern=[[1, P]], base=0, channel_multiplier=0,
                   allow_small_or_imprecise_dtypes=True).then_inc(s_pool, 1)
            g.iota(iotab[:, :], pattern=[[1, P]], base=0, channel_multiplier=0,
                   allow_small_or_imprecise_dtypes=True).then_inc(s_pool, 1)
            pool.wait_ge(s_pool, 10)
            g.affine_select(out=ident[:, :], in_=ident[:, :], compare_op=ALU.not_equal, fill=1.0, base=0,
                            pattern=[[-1, P]], channel_multiplier=1).then_inc(s_pool, 1)
            g.affine_select(out=ident4[:, :, :], in_=ident4[:, :, :], compare_op=ALU.not_equal, fill=1.0, base=0,
                            pattern=[[0, HEADS], [-1, P]], channel_multiplier=1).then_inc(s_pool, 1)
            for k in range(3):
                g.affine_select(out=pick[:, :], in_=pick[:, :], compare_op=ALU.not_equal, fill=1.0, base=-32 * k,
                                pattern=[[-1, 32]], channel_multiplier=1).then_inc(s_pool, 1)
                pool.wait_ge(s_pool, 13 + k)
            g.affine_select(out=upper[:, :], in_=upper[:, :], compare_op=ALU.is_gt, fill=0.0, base=0,
                            pattern=[[1, P]], channel_multiplier=-1).then_inc(s_pool, 1)

            with pool.Fori(0, BLOCKS // 2) as i:
                for s in range(2):
                    b = i * 2 + s
                    pool.wait_ge(h_ready, b + 1)
                    g.tensor_copy(h_res[:, bass.ds(b, 1), :].rearrange("p a d -> p (a d)"), hs[:, s, :]).then_inc(h_saved, 1)

            def gathers(sems, table, width, ready):
                pool.wait_ge(ready, 1)
                with pool.Fori(0, GROUPS // 2) as i:
                    for s in range(2):
                        gr = i * 2 + s
                        pool.wait_ge(sems["idx_ready"], gr + 1)
                        pool.wait_ge(sems["group_free"], gr + 1)
                        pool_stop(pool)
                        for c in range(CHUNKS):
                            g.indirect_dma_start(out=G[:, s, c, 0:width], out_offset=None, in_=table,
                                                 in_offset=bass.IndirectOffsetOnAxis(ap=idx[:, s, c:c + 1], axis=0)).then_inc(sems["gathered"][s], 16)

            gathers(e0, rel_table, D, tables_ready[0])
            gathers(e1, xt_table, XT, tables_ready[1])

        @block.scalar
        def _(act):
            a = nc.scalar
            act.wait_ge(s_const, 3)
            for q in range(BATCHES):
                lo, hi = q * BATCH, min((q + 1) * BATCH, BLOCKS - 1)
                act.dma_start(x_res[:, lo:hi, :], x[lo * P:hi * P, :].rearrange("(b p) d -> p b d", p=P)).then_inc(s_x, 16)
            act.dma_start(x_res[0:TAIL_ROWS, BLOCKS - 1, :], x[(BLOCKS - 1) * P:N, :]).then_inc(s_x, 16)
            act.dma_start(w_all[:, 0:R * D].rearrange("p (r e) -> p r e", r=R), W_rel.rearrange("r d e -> d r e")).then_inc(s_load, 16)
            act.dma_start(w_all[:, R * D:], W_self).then_inc(s_load, 16)
            act.dma_start(w1[:, :], W1).then_inc(s_load, 16)
            act.dma_start(w2[:, :, :], W2.rearrange("(c p) d -> p c d", p=P)).then_inc(s_load, 16)
            act.dma_start(linw[:, :, :], lin_w.rearrange("b o i -> o b i")).then_inc(s_load, 16)
            for k, v in enumerate((b_conv, g1, b1n, b2)):
                act.dma_start(rows[:, k, :], v.rearrange("(o d) -> o d", o=1).to_broadcast([P, D])).then_inc(s_load, 16)
            act.dma_start(coef[:, :], coeffs.rearrange("(o d) -> o d", o=1).to_broadcast([P, 3])).then_inc(s_load, 16)
            with nc.allow_non_contiguous_dma("small columns"):
                act.dma_start(cols[:, 0:1], g2.rearrange("(p o) -> p o", o=1)).then_inc(s_load, 16)
                act.dma_start(cols[:, 1:2], b2n.rearrange("(p o) -> p o", o=1)).then_inc(s_load, 16)
                act.dma_start(b1col[:, :], b1.rearrange("(c p) -> p c", p=P)).then_inc(s_load, 16)
                act.dma_start(linb[:, :], lin_b.rearrange("b o -> o b")).then_inc(s_load, 16)
                act.dma_start(atts[:, 0, :], att_src.rearrange("b q h c -> (q h c) b")).then_inc(s_load, 16)
                act.dma_start(atts[:, 1, :], att_dst.rearrange("b q h c -> (q h c) b")).then_inc(s_load, 16)

            act.sem_inc(xwB_sb, 2)

            def norm(b, s):
                a.activation(hs[:, s, :], x_res[:, bass.ds(b, 1), :].rearrange("p a d -> p (a d)"), ACT.Relu,
                             bias=shift_all[:, bass.ds(b, 1)], scale=rstd_all[:, bass.ds(b, 1)]).then_inc(h_ready, 1)

            act.wait_ge(h_norm, BATCHES)
            for s in range(2):
                norm(s, s)
            with act.Fori(0, BLOCKS // 2) as i:
                for s in range(2):
                    b = i * 2 + s
                    act.wait_ge(xw_ps, b + 1)
                    act.wait_ge(s_store[s], i * 32 + 16)
                    a.copy(xw[:, s, 512:R * D], banks[2 + 3 * s][:, :]).then_inc(xwB_sb, 1)
                    act.wait_ge(h_saved, b + 1)
                    norm(b + 2, s)

            def indices(sems, all_idx):
                for s in range(2):
                    a.copy(idx[:, s, :], all_idx[:, s, :]).then_inc(sems["idx_ready"], 1)

            def next_indices(sems, all_idx, i, s):
                act.wait_ge(sems["gathered"][s], i * (16 * CHUNKS) + 16 * CHUNKS)
                a.copy(idx[:, s, :], all_idx[:, bass.ds(i * 2 + (s + 2), 1), :].rearrange("p a c -> p (a c)")).then_inc(sems["idx_ready"], 1)

            act.wait_ge(s_plan, 1)
            indices(e0, idx0_all)
            with act.Fori(0, GROUPS // 2) as i:
                for s in range(2):
                    next_indices(e0, idx0_all, i, s)
            act.wait_ge(e0["idx_ready"], GROUPS + 2)

            with act.Fori(0, BATCHES) as q:
                act.wait_ge(n1_ready, q + 1)
                for j in range(BATCH):
                    a.activation(A[:, j, :], A[:, j, :], ACT.Identity, bias=shift[:, j:j + 1], scale=rstd[:, j:j + 1]).then_inc(g_in, 1)
                act.wait_ge(g_out, q * 2 + 1)
                a.activation(B[:, :, :], A[:, :, :], ACT.Gelu).then_inc(g_out, 1)
                act.wait_ge(n2_ready, q + 1)
                for j in range(BATCH):
                    a.activation(A[:, j, :], h_res[:, bass.ds(q * BATCH + j, 1), :].rearrange("p a d -> p (a d)"),
                                 ACT.Identity, bias=shift[:, j:j + 1], scale=rstd[:, j:j + 1]).then_inc(h1_ready, 1)
                for j in range(BATCH):
                    b = q * BATCH + j
                    act.wait_ge(t_ps, q * (2 * BATCH) + j + 1)
                    a.copy(tT[:, 0, :], banks[0][:, 0:P]).then_inc(t_sb, 1)
                    act.wait_ge(up_ps, b + 1)
                    for c in range(H // P):
                        a.activation(hid[:, 0, c, :], banks[1][:, c * P:(c + 1) * P], ACT.Gelu, bias=b1col[:, c:c + 1]).then_inc(up_sb, 1)
                act.wait_ge(x1_ready, q + 1)
                for j in range(BATCH):
                    a.activation(B[:, j, :], x_res[:, bass.ds(q * BATCH + j, 1), :].rearrange("p a d -> p (a d)"),
                                 ACT.Relu, bias=shift[:, j:j + 1], scale=rstd[:, j:j + 1]).then_inc(h1_ready, 1)
                for j in range(BATCH):
                    act.wait_ge(t_ps, q * (2 * BATCH) + BATCH + j + 1)
                    a.copy(tT[:, 0, :], banks[0][:, 0:P]).then_inc(t_sb, 1)

            act.sem_inc(e1["oh_ready"], 1)
            indices(e1, src_all)
            with act.Fori(0, GROUPS // 2) as i:
                for s in range(2):
                    g = i * 2 + s
                    base, windows, passes = load_plan(act, g)
                    act.wait_ge(partsT_ps, g + 1)
                    a.copy(partsT[:, :, :].rearrange("p a b -> p (a b)"), banks[6][0:96, 0:128].bitcast(bf16)).then_inc(partsT_sb, 1)
                    with act.Fori(0, windows) as w:
                        t = passes + w
                        act.wait_ge(mask_ready, t + 1)
                        act.wait_ge(e1["agg_done"], t + 1)
                        a.activation(onehot[:, :, :], mask[:, :, :], ACT.Copy, bias=1.0, scale=1.0 / BIG).then_inc(e1["oh_ready"], 1)
                        for half in range(2):
                            act.wait_ge(ohT_ps, t * 2 + half + 1)
                            a.activation(ohT[:, half * 8:half * 8 + 8, :].rearrange("p c e -> p (c e)"), banks[4 + half][:, :].bitcast(bf16),
                                         ACT.Copy, bias=1.0, scale=1.0 / BIG).then_inc(ohT_sb, 1)
                        act.wait_ge(arg_ready, t + 1)
                        a.activation(M[:, :, D:XT], z[:, :, :], ACT.Exp).then_inc(w_ready, 1)
                        act.wait_ge(marg_ready, t + 1)
                        a.activation(mexp[:, :], marg[:, :], ACT.Exp).then_inc(mexp_ready, 1)
                    next_indices(e1, src_all, i, s)

        @block.vector
        def _(dve):
            v = nc.vector
            ch = Chain(dve, c_dve)
            dve.wait_ge(s_edges, 16 * 9)
            ch.step(v.scalar_tensor_tensor(idx0_all[:, 0:GROUPS, :], src_all[:, 0:GROUPS, :], float(R), idx0_all[:, 0:GROUPS, :], ALU.mult, ALU.add))
            ch.step(v.tensor_copy(dst_all[:, :, :], dst_raw[:, :, :]))
            ch.step(v.tensor_reduce(span[:, 1, :], dst_all[:, :, :], AX.X, ALU.max))
            pad = h_res[:, 0:13, :].rearrange("p a b -> p (a b)")[:, 0:GROUPS * CHUNKS].rearrange("p (g c) -> p g c", c=CHUNKS)
            ch.step(v.tensor_scalar(pad, dst_all[:, :, :], 0.0, float(1 << 20), ALU.is_lt, ALU.mult))
            ch.step(v.tensor_tensor(pad, pad, dst_all[:, :, :], ALU.add))
            ch.step(v.tensor_reduce(span[:, 0, :], pad, AX.X, ALU.min))
            dve.sem_inc(s_setdve, 1)
            dve.wait_ge(s_setpe, 1)
            ch.step(v.tensor_reduce(spanc[:, 0:1], banks[0][0:GROUPS, 0:P], AX.X, ALU.min))
            ch.step(v.tensor_reduce(spanc[:, 1:2], banks[0][0:GROUPS, P:2 * P], AX.X, ALU.max))
            ch.step(v.tensor_tensor(spani[:, :], spanc[:, 1:2], spanc[:, 0:1], ALU.subtract))
            ch.step(v.tensor_scalar(spani[:, :], spani[:, :], 7, None, ALU.arith_shift_right))
            ch.step(v.tensor_scalar(spanc[:, 2:3], spani[:, :], 1.0, None, ALU.add))
            dve.sem_inc(s_setdve, 1)
            dve.wait_ge(s_setpe, 2)
            ch.step(v.tensor_copy(base_all[:, :], banks[1][:, 0:GROUPS]))
            for k in range(3):
                ch.step(v.tensor_copy(plan[:, :, k], banks[1][0:1, k * GROUPS:(k + 1) * GROUPS]))
            ch.step(v.tensor_copy(tmp[0:1, 0:1], banks[1][0:1, 2 * GROUPS - 1:2 * GROUPS]))
            ch.step(v.tensor_tensor(plan[:, 0, 3:4], tmp[0:1, 0:1], banks[1][0:1, 3 * GROUPS - 1:3 * GROUPS], ALU.add))
            dve.sem_inc(s_plan, 1)

            dve.wait_ge(s_load, 16 * 16)
            dve.wait_ge(s_pool, 16)
            for dstt, srct in ((wcomb[:, :], [linw[:, k, :] for k in range(3)]), (bcomb[:, :], [linb[:, k:k + 1] for k in range(3)]),
                               (acomb[:, 0:1], [atts[:, 0, k:k + 1] for k in range(3)]), (acomb[:, 1:2], [atts[:, 1, k:k + 1] for k in range(3)])):
                ch.step(v.tensor_scalar(dstt, srct[0], coef[:, 0:1], None, ALU.mult))
                for k in (1, 2):
                    ch.step(v.scalar_tensor_tensor(dstt, srct[k], coef[:, k:k + 1], dstt, ALU.mult, ALU.add))
            ch.step(v.tensor_copy(a8[:, 0:D], ident[:, :]))
            for k in range(2):
                for hd in range(HEADS):
                    ch.step(v.tensor_copy(a8[hd * HC:(hd + 1) * HC, D + k * HEADS + hd:D + k * HEADS + hd + 1],
                                          acomb[hd * HC:(hd + 1) * HC, k:k + 1]))
            dve.sem_inc(s_setdve, 1)
            dve.wait_ge(s_setpe, 3)
            ch.step(v.tensor_copy(wx[:, :], banks[0][:, 0:XT + HEADS]))
            ch.step(v.tensor_copy(bx[:, :], banks[1][:, 0:XT + HEADS]))
            ch.step(v.tensor_tensor(b1col[:, :], b1col[:, :], banks[2][:, 0:H // P], ALU.add))
            ch.step(v.tensor_scalar(w1[:, :], w1[:, :], cols[:, 0:1], None, ALU.mult))
            dve.sem_inc(s_setdve, 1)

            n0 = ch.n
            dve.wait_ge(s_x, 16 * (BATCHES + 1))
            dve.wait_ge(s_const, 3)
            with dve.Fori(0, BATCHES) as q:
                c = Chain(dve, c_dve, q * STATS_STEPS + n0)
                stats_steps(nc, c, dve_stop, [x_res[:, bass.ds(q * BATCH + j, 1), :].rearrange("p a d -> p (a d)") for j in range(BATCH)],
                            stats, mv, None, var[:, :], tmp[:, :], rstd_all[:, bass.ds(q * BATCH, BATCH)], shift_all[:, bass.ds(q * BATCH, BATCH)])
                dve.sem_inc(h_norm, 1)
            assert c.n == STATS_STEPS, c.n

            dve.sem_inc(xwA_sb, 2)
            with dve.Fori(0, BLOCKS // 2) as i:
                for s in range(2):
                    b = i * 2 + s
                    dve.wait_ge(hT_ps, b + 1)
                    v.tensor_copy(hT[:, s, :], banks[0][:, s * P:(s + 1) * P]).then_inc(hT_sb, 1)
                    dve.wait_ge(xw_ps, b + 1)
                    dve.wait_ge(s_store[s], i * 32 + 16)
                    v.tensor_tensor(xw[:, s, R * D:], banks[3 + 3 * s][:, 0:D], rows[:, 0, :], ALU.add)
                    v.tensor_copy(xw[:, s, 0:512], banks[1 + 3 * s][:, :]).then_inc(xwA_sb, 1)

            def window(sems, c, g):
                c.step(v.tensor_scalar(rel[:, :], rel[:, :], -float(P), None, ALU.add))
                for k in range(CHUNKS):
                    ins = v.tensor_scalar(onehot[:, k, :], iota[:, :], rel[:, k:k + 1], None, ALU.is_equal)
                ins.then_inc(sems["oh_ready"], 1)

            def mask_window(sems, c):
                c.step(v.tensor_scalar(rel[:, :], rel[:, :], -float(P), None, ALU.add))
                for k in range(CHUNKS):
                    ins = v.tensor_scalar(mask[:, k, :], iotab[:, :], rel[:, k:k + 1], -BIG, ALU.not_equal, ALU.mult)
                ins.then_inc(mask_ready, 1)

            def first_rel(sems, g):
                v.tensor_scalar(rel[:, :], dst_all[:, bass.ds(g, 1), :].rearrange("p a c -> p (a c)"),
                                base_all[:, bass.ds(g, 1)], float(P), ALU.subtract, ALU.add).then_inc(sems["chain"], 1)

            dve.sem_inc(e0["merged"], 1)
            with dve.Fori(0, GROUPS) as g:
                base, windows, passes = load_plan(dve, g)
                first_rel(e0, g)
                dve.wait_ge(e0["chain"], passes + g + 1)
                dve_stop(dve)
                with dve.Fori(0, windows) as w:
                    t = passes + w
                    window(e0, Chain(dve, e0["chain"], t + g + 1), g)
                    dve.wait_ge(e0["agg_done"], t + 1)
                    dve.wait_ge(e0["old_ready"], (t + 1) * 16)
                    v.tensor_tensor(new[:, 0:D], banks[7][:, 0:D], old[:, 0:D], ALU.add).then_inc(e0["merged"], 1)

            DENSE = STATS_STEPS * 3 + 3
            dve.sem_inc(x2_ready, 1)
            with dve.Fori(0, BATCHES) as q:
                c = Chain(dve, c_dense, q * DENSE)
                hb = h_res[:, bass.ds(q * BATCH, BATCH), :]
                xb = x_res[:, bass.ds(q * BATCH, BATCH), :]
                dve.wait_ge(a_load, q * 16 + 16)
                stats_steps(nc, c, dve_stop, [A[:, j, :] for j in range(BATCH)], stats, mv, None, var[:, :], tmp[:, :], rstd[:, :], shift[:, :])
                dve.sem_inc(n1_ready, 1)
                dve.wait_ge(g_in, q * BATCH + BATCH)
                c.step(v.tensor_tensor(A[:, :, :], A[:, :, :], rows[:, 1:2, :].to_broadcast([P, BATCH, D]), ALU.mult))
                v.tensor_tensor(A[:, :, :], A[:, :, :], rows[:, 2:3, :].to_broadcast([P, BATCH, D]), ALU.add).then_inc(g_out, 1)
                dve.wait_ge(g_out, q * 2 + 2)
                c.step(v.tensor_tensor(hb, hb, B[:, :, :], ALU.add))
                stats_steps(nc, c, dve_stop, [h_res[:, bass.ds(q * BATCH + j, 1), :].rearrange("p a d -> p (a d)") for j in range(BATCH)],
                            stats, mv, None, var[:, :], tmp[:, :], rstd[:, :], shift[:, :])
                dve.sem_inc(n2_ready, 1)
                c.step(v.tensor_tensor(xb, xb, hb, ALU.add))
                dve_stop(dve)
                with dve.Fori(0, BATCH) as j:
                    b = q * BATCH + j
                    dve.wait_ge(down_ps, b + 1)
                    v.tensor_tensor(B[:, bass.ds(j, 1), :].rearrange("p a d -> p (a d)"), banks[2][:, 0:D], rows[:, 3, :], ALU.add).then_inc(ff_ready, 1)
                dve.wait_ge(ff_ready, q * (BATCH + 1) + BATCH)
                v.tensor_tensor(xb, xb, B[:, :, :], ALU.add).then_inc(ff_ready, 1)
                dve.wait_ge(ff_ready, q * (BATCH + 1) + BATCH + 1)
                stats_steps(nc, c, dve_stop, [x_res[:, bass.ds(q * BATCH + j, 1), :].rearrange("p a d -> p (a d)") for j in range(BATCH)],
                            stats, mv, None, var[:, :], tmp[:, :], rstd[:, :], shift[:, :])
                dve.sem_inc(x1_ready, 1)
                dve.sem_inc(x2_ready, 1)
                with dve.Fori(0, BATCH) as j:
                    b = q * BATCH + j
                    dve.wait_ge(xt_ps, b + 1)
                    v.tensor_tensor(xt_sbuf[:, 0, :], banks[3][:, 0:XT + HEADS], bx[:, :], ALU.add).then_inc(xt_sb, 1)
                    dve.wait_ge(s_xt, b * 32 + 32)
            assert c.n == DENSE, c.n

            for k, tile in enumerate((old[:, :], new[:, :], mexp[:, :], banks[7][:, 0:XT])):
                v.memset(tile, 0.0).then_inc(merge_chain, 1)
            dve.wait_ge(merge_chain, 4)

            def merge(t):
                c = Chain(dve, merge_chain, t * 4 + 4)
                c.step(v.tensor_tensor(scaled[:, 0:D].rearrange("p (h k) -> p h k", h=HEADS), old[:, 0:D].rearrange("p (h k) -> p h k", h=HEADS),
                                       mexp[:, 0:HEADS].rearrange("p (h o) -> p h o", o=1).to_broadcast([P, HEADS, HC]), ALU.mult))
                c.step(v.tensor_tensor(scaled[:, D:XT], old[:, D:XT], mexp[:, 0:HEADS], ALU.mult))
                dve.wait_ge(e1["agg_done"], t + 1)
                c.step(v.tensor_tensor(new[:, 0:D].rearrange("p (h k) -> p h k", h=HEADS), banks[7][:, 0:D].rearrange("p (h k) -> p h k", h=HEADS),
                                       mexp[:, HEADS:].rearrange("p (h o) -> p h o", o=1).to_broadcast([P, HEADS, HC]), ALU.mult))
                c.step(v.tensor_tensor(new[:, D:XT], banks[7][:, D:XT], mexp[:, HEADS:], ALU.mult))
                v.tensor_tensor(new[:, 0:XT], new[:, 0:XT], scaled[:, :], ALU.add).then_inc(e1["merged"], 1)

            GSTEPS, PSTEPS = 5, 19
            with dve.Fori(0, GROUPS // 2) as i:
                for s in range(2):
                    g = i * 2 + s
                    base, windows, passes = load_plan(dve, g)
                    c = Chain(dve, e1["chain"], passes * PSTEPS + g * GSTEPS)
                    c.step(v.tensor_scalar(rel[:, :], dst_all[:, bass.ds(g, 1), :].rearrange("p a c -> p (a c)"),
                                           base_all[:, bass.ds(g, 1)], float(P), ALU.subtract, ALU.add))
                    dve.wait_ge(e1["gathered"][s], i * (16 * CHUNKS) + 16 * CHUNKS)
                    for k in range(2):
                        c.step(v.tensor_copy(parts[:, k, 0, :].rearrange("p (c h) -> p c h", h=HEADS), G[:, s, k * 8:k * 8 + 8, D:XT]))
                    for k in range(2):
                        v.tensor_tensor(resid[:, k, :].rearrange("p (c h) -> p c h", h=HEADS), G[:, s, k * 8:k * 8 + 8, D:XT],
                                        parts[:, k, 0, :].rearrange("p (c h) -> p c h", h=HEADS), ALU.subtract).then_inc(e1["chain"], 1)
                    c.n += 2
                    dve.wait_ge(e1["chain"], c.base + c.n)
                    assert c.n == 5
                    c2 = Chain(dve, split_chain, g * 2)
                    c2.step(v.tensor_copy(parts[:, :, 1, :], resid[:, :, :]))
                    c2.step(v.tensor_tensor(resid[:, :, :], resid[:, :, :], parts[:, :, 1, :], ALU.subtract))
                    v.tensor_copy(parts[:, :, 2, :], resid[:, :, :]).then_inc(parts_ready, 1)
                    dve_stop(dve)
                    with dve.Fori(0, windows) as w:
                        t = passes + w
                        c = Chain(dve, e1["chain"], t * PSTEPS + g * GSTEPS + GSTEPS)
                        dve.wait_ge(e1["oh_ready"], t + 1)
                        mask_window(e1, c)
                        merge(t)
                        for k in range(CHUNKS // 2):
                            dve.wait_ge(score_ps, t * (CHUNKS // 2) + k + 1)
                            v.tensor_reduce(mk[:, 2 * k:2 * k + 2, :], score[k % 2], AX.X, ALU.max).then_inc(score_used, 1)
                        dve.wait_ge(score_used, t * (CHUNKS // 2) + CHUNKS // 2 + 2)
                        dve.wait_ge(ad_ready, (t + 1) * 16)
                        c.step(v.tensor_reduce(mg[:, :], mk[:, :, :].rearrange("p c h -> p h c"), AX.X, ALU.max))
                        c.step(v.tensor_tensor(cc[:, 0, :], mg[:, :], adw[:, :], ALU.add))
                        c.step(v.tensor_copy(ca[:, HEADS:], adw[:, :]))
                        c.step(v.scalar_tensor_tensor(ca[:, 0:HEADS], cc[:, 0, :], 0.2, cc[:, 0, :], ALU.mult, ALU.max))
                        c.step(v.tensor_copy(cparts[:, 0, :], ca[:, :]))
                        c.step(v.tensor_tensor(cres[:, :], ca[:, :], cparts[:, 0, :], ALU.subtract))
                        c.step(v.tensor_copy(cparts[:, 1, :], cres[:, :]))
                        c.step(v.tensor_tensor(cres[:, :], cres[:, :], cparts[:, 1, :], ALU.subtract))
                        v.tensor_copy(cparts[:, 2, :], cres[:, :]).then_inc(c_ready, 1)
                        dve.wait_ge(c_ps, t + 1)
                        cb = cbs[:, :, :]
                        c.step(v.tensor_reduce(cb, banks[6][:, 128:128 + CHUNKS * 24].rearrange("p (c k j) -> p c j k", k=3, j=8), AX.X, ALU.add))
                        c.step(v.tensor_tensor(z[:, :, :], cb[:, :, HEADS:], G[:, s, :, D:XT], ALU.add))
                        c.step(v.scalar_tensor_tensor(z2[:, :, :], z[:, :, :], 0.2, z[:, :, :], ALU.mult, ALU.max))
                        c.step(v.tensor_tensor(z2[:, :, :], z2[:, :, :], cb[:, :, 0:HEADS], ALU.subtract))
                        v.tensor_scalar(z[:, :, :], z2[:, :, :], 0.0, None, ALU.min).then_inc(arg_ready, 1)
                        dve.wait_ge(w_ready, t + 1)
                        for lo in (0, 8):
                            v.tensor_tensor(M[:, lo:lo + 8, 0:D].rearrange("p c (h k) -> p c h k", h=HEADS),
                                            G[:, s, lo:lo + 8, 0:D].rearrange("p c (h k) -> p c h k", h=HEADS),
                                            M[:, lo:lo + 8, D:XT].rearrange("p c (h o) -> p c h o", o=1).to_broadcast([P, 8, HEADS, HC]),
                                            ALU.mult).then_inc(msg_ready, 1)
                        dve.wait_ge(e1["old_ready"], (t + 1) * 16)
                        c.step(v.tensor_tensor(new[:, XT:], old[:, XT:], mg[:, :], ALU.max))
                        c.step(v.tensor_tensor(cc[:, 1, :], new[:, XT:], adw[:, :], ALU.add))
                        c.step(v.scalar_tensor_tensor(cc[:, 2, :], cc[:, 1, :], 0.2, cc[:, 1, :], ALU.mult, ALU.max))
                        c.step(v.tensor_tensor(cc[:, 3, :], old[:, XT:], adw[:, :], ALU.add))
                        c.step(v.scalar_tensor_tensor(cc[:, 4, :], cc[:, 3, :], 0.2, cc[:, 3, :], ALU.mult, ALU.max))
                        c.step(v.tensor_tensor(marg[:, 0:HEADS], cc[:, 4, :], cc[:, 2, :], ALU.subtract))
                        v.tensor_tensor(marg[:, HEADS:], ca[:, 0:HEADS], cc[:, 2, :], ALU.subtract).then_inc(marg_ready, 1)
                        dve.wait_ge(mexp_ready, t + 1)
                        assert c.n == PSTEPS, c.n
                    dve.wait_ge(msg_ready, (passes + windows) * 2)
                    dve.sem_inc(e1["group_free"], 1)
            merge(dve.value_load(plan[0:1, 0:1, 3:4], min_val=1, max_val=GROUPS * BLOCKS))

            ch = Chain(dve, c_fin)
            for q in range(BATCHES):
                s = q % 2
                lo = q * BATCH
                f = fin[:, s, 0:BATCH * XT].rearrange("p (b c) -> p b c", c=XT)
                dve.wait_ge(fin_load[s], 16 * (q // 2 + 1))
                ch.step(v.tensor_scalar(f[:, :, D:XT], f[:, :, D:XT], 1e-16, None, ALU.add))
                ch.step(v.reciprocal(f[:, :, D:XT], f[:, :, D:XT]))
                ch.step(v.tensor_tensor(f[:, :, 0:D].rearrange("p b (h k) -> p b h k", h=HEADS), f[:, :, 0:D].rearrange("p b (h k) -> p b h k", h=HEADS),
                                        f[:, :, D:XT].rearrange("p b (h o) -> p b h o", o=1).to_broadcast([P, BATCH, HEADS, HC]), ALU.mult))
                v.tensor_tensor(x_res[:, lo:lo + BATCH, :], x_res[:, lo:lo + BATCH, :], f[:, :, 0:D], ALU.add).then_inc(fin_done, 1)

        @block.tensor
        def _(pe):
            t = nc.tensor
            pe.wait_ge(s_pool, 16)
            pe.wait_ge(s_setdve, 1)
            t.transpose(banks[0][0:GROUPS, 0:P], span[:, 0, :], ident[:, :])
            t.transpose(banks[0][0:GROUPS, P:2 * P], span[:, 1, :], ident[:, :]).then_inc(s_setpe, 1)
            pe.wait_ge(s_setdve, 2)
            t.matmul(banks[1][:, 0:GROUPS], spanc[:, 0:1].to_broadcast([GROUPS, P]), ident[0:GROUPS, 0:GROUPS], start=True, stop=True)
            t.matmul(banks[1][:, GROUPS:2 * GROUPS], spanc[:, 2:3].to_broadcast([GROUPS, P]), ident[0:GROUPS, 0:GROUPS], start=True, stop=True)
            t.matmul(banks[1][:, 2 * GROUPS:3 * GROUPS], spanc[:, 2:3].to_broadcast([GROUPS, P]), upper[0:GROUPS, 0:GROUPS], start=True, stop=True).then_inc(s_setpe, 1)
            pe.wait_ge(s_setdve, 3)
            t.matmul(banks[0][:, 0:XT + HEADS], wcomb[:, :], a8[:, :], start=True, stop=True)
            t.matmul(banks[1][:, 0:XT + HEADS], bcomb[:, 0:1].to_broadcast([P, P]), a8[:, :], start=True, stop=True)
            for c in range(H // P):
                ins = t.matmul(banks[2][:, c:c + 1], w1[:, c * P:(c + 1) * P], cols[:, 1:2], start=True, stop=True)
            ins.then_inc(s_setpe, 1)
            pe.wait_ge(s_setdve, 4)

            with pe.Fori(0, BLOCKS // 2) as i:
                for s in range(2):
                    b = i * 2 + s
                    pe.wait_ge(h_ready, b + 1)
                    pe.wait_ge(xwA_sb, b + 1)
                    pe.wait_ge(xwB_sb, b + 1)
                    t.transpose(banks[0][:, s * P:(s + 1) * P], hs[:, s, :], ident[:, :]).then_inc(hT_ps, 1)
                    pe.wait_ge(hT_sb, b + 1)
                    t.matmul(banks[1 + 3 * s][:, :], hT[:, s, :], w_all[:, 0:512], start=True, stop=True)
                    t.matmul(banks[2 + 3 * s][:, :], hT[:, s, :], w_all[:, 512:1024], start=True, stop=True)
                    t.matmul(banks[3 + 3 * s][:, 0:D], hT[:, s, :], w_all[:, R * D:], start=True, stop=True).then_inc(xw_ps, 1)

            pe.sem_inc(e0["group_free"], 2)
            with pe.Fori(0, GROUPS // 2) as i:
                for s in range(2):
                    g = i * 2 + s
                    base, windows, passes = load_plan(pe, g)
                    pe.wait_ge(e0["gathered"][s], i * (16 * CHUNKS) + 16 * CHUNKS)
                    pe_stop(pe)
                    with pe.Fori(0, windows) as w:
                        tt = passes + w
                        pe.wait_ge(e0["oh_ready"], tt + 1)
                        pe.wait_ge(e0["merged"], tt + 1)
                        for k in range(CHUNKS):
                            ins = t.matmul(banks[7][:, 0:D], onehot[:, k, :], G[:, s, k, 0:D], start=(k == 0), stop=(k == CHUNKS - 1))
                        ins.then_inc(e0["agg_done"], 1)
                    pe.wait_ge(e0["agg_done"], passes + windows)
                    pe.sem_inc(e0["group_free"], 1)

            with pe.Fori(0, BATCHES) as q:
                pe.wait_ge(h1_ready, q * (2 * BATCH) + BATCH)
                for j in range(BATCH):
                    b = q * BATCH + j
                    t.transpose(banks[0][:, 0:P], A[:, j, :], ident[:, :]).then_inc(t_ps, 1)
                    pe.wait_ge(t_sb, q * (2 * BATCH) + j + 1)
                    for c in range(H // P):
                        ins = t.matmul(banks[1][:, c * P:(c + 1) * P], w1[:, c * P:(c + 1) * P], tT[:, 0, :], start=True, stop=True)
                    ins.then_inc(up_ps, 1)
                    pe.wait_ge(up_sb, b * (H // P) + H // P)
                    for c in range(H // P):
                        ins = t.matmul(banks[2][:, 0:D], hid[:, 0, c, :], w2[:, c, :], start=(c == 0), stop=(c == H // P - 1))
                    ins.then_inc(down_ps, 1)
                    pe.wait_ge(ff_ready, q * (BATCH + 1) + j + 1)
                pe.wait_ge(h1_ready, q * (2 * BATCH) + 2 * BATCH)
                for j in range(BATCH):
                    b = q * BATCH + j
                    t.transpose(banks[0][:, 0:P], B[:, j, :], ident[:, :]).then_inc(t_ps, 1)
                    pe.wait_ge(t_sb, q * (2 * BATCH) + BATCH + j + 1)
                    t.matmul(banks[3][:, 0:XT + HEADS], tT[:, 0, :], wx[:, :], start=True, stop=True).then_inc(xt_ps, 1)
                    pe.wait_ge(xt_sb, b + 1)

            pe.sem_inc(e1["group_free"], 2)
            pe.sem_inc(e1["agg_done"], 1)
            pe.sem_inc(score_used, 2)
            with pe.Fori(0, GROUPS // 2) as i:
                for s in range(2):
                    g = i * 2 + s
                    base, windows, passes = load_plan(pe, g)
                    pe.wait_ge(parts_ready, g + 1)
                    for half in range(2):
                        ins = t.transpose(banks[6][0:96, half * 64:half * 64 + 64].bitcast(bf16), parts[:, half, :, :].rearrange("p a b -> p (a b)"), ident4[:, 0, :])
                    ins.then_inc(partsT_ps, 1)
                    pe.wait_ge(partsT_sb, g + 1)
                    pe.wait_ge(e1["gathered"][s], i * (16 * CHUNKS) + 16 * CHUNKS)
                    pe_stop(pe)
                    with pe.Fori(0, windows) as w:
                        tt = passes + w
                        pe.wait_ge(mask_ready, tt + 1)
                        for kp in range(CHUNKS // 2):
                            pe.wait_ge(score_used, tt * (CHUNKS // 2) + kp + 1)
                            for k in (2 * kp, 2 * kp + 1):
                                half, kk = divmod(k, 8)
                                dstp = score[kp % 2][:, k % 2, :, :]
                                for hd in range(HEADS):
                                    q = kk * HEADS + hd
                                    t.matmul(dstp[:, hd, :], pick[:, q:q + 1].to_broadcast([96, P]), partsT[:, half, :],
                                             start=(hd == 0), stop=False)
                                ins = t.matmul(dstp, mask[:, k, :], ident4[:, :, :], start=False, stop=True)
                            ins.then_inc(score_ps, 1)
                        for half in range(2):
                            for k in range(8):
                                ins = t.transpose(banks[4 + half][:, k * 64:k * 64 + 64].bitcast(bf16), mask[:, half * 8 + k, :], ident4[:, 0, :])
                            ins.then_inc(ohT_ps, 1)
                        pe.wait_ge(ohT_sb, tt * 2 + 2)
                        pe.wait_ge(c_ready, tt + 1)
                        for k in range(CHUNKS):
                            ins = t.matmul(banks[6][:, 128 + k * 24:152 + k * 24], ohT[:, k, :], cparts[:, :, :].rearrange("p a b -> p (a b)"), start=True, stop=True)
                        ins.then_inc(c_ps, 1)
                        pe.wait_ge(e1["oh_ready"], tt + 2)
                        pe.wait_ge(e1["merged"], tt + 1)
                        for k in range(CHUNKS):
                            if k % 8 == 0:
                                pe.wait_ge(msg_ready, tt * 2 + k // 8 + 1)
                            ins = t.matmul(banks[7][:, 0:XT], onehot[:, k, :], M[:, k, :], start=(k == 0), stop=(k == CHUNKS - 1))
                        ins.then_inc(e1["agg_done"], 1)


_INS = ["x", "src", "dst", "edge_type_8", "L0_gnn_W_rel", "L0_gnn_W_self", "L0_gnn_b_conv", "L0_gnn_ln1_g", "L0_gnn_ln1_b",
        "L0_gnn_ln2_g", "L0_gnn_ln2_b", "L0_gnn_W1", "L0_gnn_b1", "L0_gnn_W2", "L0_gnn_b2", "L1_gnn_coeffs_t",
        "L1_gnn_lin_weight", "L1_gnn_lin_bias", "L1_gnn_att_src", "L1_gnn_att_dst"]


def kernel(**inputs):
    import numpy as _np
    import concourse.bacc as _bacc
    from concourse import mybir as _mybir
    from concourse.bass_utils import run_bass_kernel_spmd as _run

    nc = _bacc.Bacc("TRN2", target_bir_lowering=False, num_devices=1)
    arrays, args = {}, []
    for name in _INS:
        a = _np.ascontiguousarray(inputs[name])
        arrays[f"in_{name}"] = a
        args.append(nc.dram_tensor(f"in_{name}", a.shape, _mybir.dt.from_np(a.dtype), kind="ExternalInput").ap())
    out = nc.dram_tensor("out_0", (N, D), _mybir.dt.float32, kind="ExternalOutput").ap()
    build(nc, *args, out)
    r = _run(nc, [arrays], core_ids=[0])
    return r.results[0]["out_0"]
```

```python
import concourse.bass as bass
import numpy as np
from concourse import mybir
from contextlib import ExitStack

P = 128
N, E, D, R, H = 12500, 212500, 128, 8, 512
HEADS, HC = 4, 32
BLOCKS = -(-N // P)
TAIL_ROWS = N - (BLOCKS - 1) * P
CHUNKS = 16
GROUP = CHUNKS * P
GROUPS = -(-E // GROUP)
LAST_FULL = (E - (GROUPS - 1) * GROUP) // CHUNKS
LAST_REST = (E - (GROUPS - 1) * GROUP) % CHUNKS
PAD_ROWS = (BLOCKS + 1) * P
BATCH = 7
BATCHES = BLOCKS // BATCH
SPARE = BATCH
AGG_ROWS = (BLOCKS + 2 * BATCH) * P
XT = D + HEADS
ST = D + 2 * HEADS
BIG = float(2.0 ** 100)
SLICES = (0, 2, 8, CHUNKS)
EPS = 1e-5
MAGIC = float(0x5F3759DF)
NEWTON = 3
assert BLOCKS % BATCH == 0 and GROUPS % 2 == 0 and BLOCKS % 2 == 0

f32, bf16 = mybir.dt.float32, mybir.dt.bfloat16
i32, u32 = mybir.dt.int32, mybir.dt.uint32
ALU = mybir.AluOpType
ACT = mybir.ActivationFunctionType
AX = mybir.AxisListType


class Chain:

    def __init__(self, eng, sem, base=0):
        self.eng, self.sem, self.base, self.n = eng, sem, base, 0

    def step(self, ins):
        self.beside(ins)
        self.wait()

    def beside(self, ins):
        self.n += 1
        ins.then_inc(self.sem, 1)

    def wait(self):
        self.eng.wait_ge(self.sem, self.base + self.n)


class Stops:

    def __init__(self, sem):
        self.sem = sem

    def __call__(self, eng):
        eng.sem_inc(self.sem, 1)


RSQRT_STEPS = 3 + 4 * NEWTON


def rsqrt_steps(nc, chain, out, var, tmp):
    v = nc.vector
    chain.step(v.tensor_scalar(tmp, var, EPS, None, ALU.add))
    chain.step(v.tensor_scalar(out.bitcast(i32), tmp.bitcast(i32), 1, None, ALU.arith_shift_right))
    chain.step(v.tensor_scalar(out.bitcast(i32), out.bitcast(i32), -1.0, MAGIC, ALU.mult, ALU.add))
    for _ in range(NEWTON):
        sq = var
        chain.step(v.tensor_tensor(sq, out, out, ALU.mult))
        chain.step(v.tensor_tensor(sq, sq, tmp, ALU.mult))
        chain.step(v.tensor_scalar(sq, sq, -0.5, 1.5, ALU.mult, ALU.add))
        chain.step(v.tensor_tensor(out, out, sq, ALU.mult))


STATS_STEPS = 2 + RSQRT_STEPS + 2


def stats_steps(nc, chain, stop, rows, stats, mv, mean, var, tmp, rstd, shift):
    v = nc.vector
    n = len(rows)
    stop(chain.eng)
    for j, row in enumerate(rows[:-1]):
        v.bn_stats(stats[:, j, :], row)
    chain.step(v.bn_stats(stats[:, n - 1, :], rows[-1]))
    stop(chain.eng)
    for j in range(n - 1):
        v.bn_aggr(mv[:, j, :], stats[:, j, :])
    chain.step(v.bn_aggr(mv[:, n - 1, :], stats[:, n - 1, :]))
    chain.step(v.tensor_copy(var, mv[:, :, 1]))
    rsqrt_steps(nc, chain, rstd, var, tmp)
    chain.step(v.scalar_tensor_tensor(shift, mv[:, :, 0], -1.0, rstd, ALU.mult, ALU.mult))


def build(nc, x, src, dst, typ, W_rel, W_self, b_conv, g1, b1n, g2, b2n, W1, b1, W2, b2,
          coeffs, lin_w, lin_b, att_src, att_dst, out):
    dram = lambda name, shape, dt=f32: nc.dram_tensor(name, shape, dt).ap()
    rel_table = dram("rel_table", (BLOCKS * P * R, D))
    agg_state = dram("agg_state", (AGG_ROWS, D))
    xt_table = dram("xt_table", (PAD_ROWS, XT))
    ad_table = dram("ad_table", (PAD_ROWS, HEADS))
    att_state = dram("att_state", (PAD_ROWS, ST))

    ctx = ExitStack()
    with ctx:
        sb = lambda name, shape, dt=f32: ctx.enter_context(nc.sbuf_tensor(name, shape, dt))
        pb = lambda name, shape, dt=f32: ctx.enter_context(nc.psum_tensor(name, shape, dt))
        sem = lambda name: ctx.enter_context(nc.semaphore(name))

        ident = sb("ident", [P, P])
        ident4 = sb("ident4", [P, HEADS, P], bf16)
        iota = sb("iota", [P, P])
        pick = sb("pick", [96, 32], bf16)
        upper = sb("upper", [P, P])
        zeros = sb("zeros", [P, ST])
        w_all = sb("w_all", [P, R * D + D])
        w1 = sb("w1", [P, H])
        w2 = sb("w2", [P, H // P, D])
        b1col = sb("b1col", [P, H // P])
        wx = sb("wx", [P, XT + HEADS])
        bx = sb("bx", [P, XT + HEADS])
        rows = sb("rows", [P, 4, D])
        cols = sb("cols", [P, 2])
        linw = sb("linw", [P, 3, D])
        linb = sb("linb", [P, 3])
        atts = sb("atts", [P, 2, 3])
        coef = sb("coef", [P, 3])
        wcomb = sb("wcomb", [P, D])
        acomb = sb("acomb", [P, 2])
        bcomb = sb("bcomb", [P, 1])
        a8 = sb("a8", [P, D + 2 * HEADS])

        x_res = sb("x_res", [P, BLOCKS + SPARE, D])
        h_res = sb("h_res", [P, BLOCKS + SPARE, D])
        src_all = sb("src_all", [P, GROUPS + 2, CHUNKS], i32)
        idx0_all = sb("idx0_all", [P, GROUPS + 2, CHUNKS], i32)
        dst_raw = sb("dst_raw", [P, GROUPS, CHUNKS], i32)
        dst_all = sb("dst_all", [P, GROUPS, CHUNKS])
        span = sb("span", [P, 2, GROUPS])
        spanc = sb("spanc", [GROUPS, 4])
        spani = sb("spani", [GROUPS, 1], i32)
        base_all = sb("base_all", [P, GROUPS])
        plan = sb("plan", [1, GROUPS, 4], i32)

        stats = sb("stats", [P, BATCH, 6])
        mv = sb("mv", [P, BATCH, 2])
        var = sb("var", [P, BATCH])
        tmp = sb("tmp", [P, BATCH])
        rstd = sb("rstd", [P, BATCH])
        shift = sb("shift", [P, BATCH])
        rstd_all = sb("rstd_all", [P, BLOCKS + 2])
        shift_all = sb("shift_all", [P, BLOCKS + 2])
        hs = sb("hs", [P, 2, D])
        hT = sb("hT", [P, 2, D])
        xw = sb("xw", [P, 2, R * D + D])

        idx = sb("idx", [P, 2, CHUNKS], u32)
        rel = sb("rel", [P, CHUNKS])
        G = sb("G", [P, 2, CHUNKS, XT])
        onehot = sb("onehot", [P, CHUNKS, P])
        old = sb("old", [P, ST])
        new = sb("new", [P, ST])

        rstd3 = [sb(f"rstd{k}", [P, BATCH]) for k in range(3)]
        shift3 = [sb(f"shift{k}", [P, BATCH]) for k in range(3)]

        pairs = [pb(f"pair{i}", [P, 1024]) for i in range(2)]
        banks = [pairs[i // 2][:, (i % 2) * 512:(i % 2) * 512 + 512] for i in range(4)] + \
                [pb(f"bank{i}", [P, 512])[:, :] for i in range(4, 8)]
        score = [pr[:, :].rearrange("p (c h e) -> p c h e", c=2, h=HEADS) for pr in pairs]

        s_const, s_pool, s_load, s_x, s_edges = (sem(n) for n in ("s_const", "s_pool", "s_load", "s_x", "s_edges"))
        s_edges_set, s_set, s_setpe, s_setdve, s_plan = (sem(n) for n in ("s_edges_set", "s_set", "s_setpe", "s_setdve", "s_plan"))
        c_dve = sem("c_dve")
        h_norm, h_ready, h_saved, hT_ps, hT_sb, xw_ps, xwA_sb, xwB_sb = (sem(n) for n in (
            "h_norm", "h_ready", "h_saved", "hT_ps", "hT_sb", "xw_ps", "xwA_sb", "xwB_sb"))
        s_store = [sem("s_store0"), sem("s_store1")]
        s_agg = sem("s_agg")
        ff_ready, split_chain = sem("ff_ready"), sem("split_chain")

        def edge_sems(k):
            n = dict(idx_ready=sem(f"idx_ready{k}"), gathered=[sem(f"gathered{k}_{i}") for i in range(2)],
                     group_free=sem(f"group_free{k}"), oh_ready=sem(f"oh_ready{k}"), agg_done=sem(f"agg_done{k}"),
                     merged=sem(f"merged{k}"), old_ready=sem(f"old_ready{k}"), chain=sem(f"chain{k}"))
            return n

        e0, e1 = edge_sems(0), edge_sems(1)
        att_stored = sem("att_stored")
        tables_ready = [sem("tables_ready0"), sem("tables_ready1")]

        c_dense = sem("c_dense")
        a_load, s_xt = ([sem(f"{n}{k}") for k in range(2)] for n in ("a_load", "s_xt"))
        n_ready = [sem(f"n_ready{k}") for k in range(3)]
        (norm1_done, norm2_done, norm3_done, affine_done, gelu_done, hadd_done, xadd_done, t_ps, t_sb, up_ps, up_sb,
         down_ps, xt_ps, xt_sb) = (sem(n) for n in (
             "norm1_done", "norm2_done", "norm3_done", "affine_done", "gelu_done", "hadd_done", "xadd_done", "t_ps", "t_sb",
             "up_ps", "up_sb", "down_ps", "xt_ps", "xt_sb"))
        affine_half = sem("affine_half")

        ad_ready, mask_ready, parts_ready, partsT_ps, partsT_sb, ohT_ps, ohT_sb, score_ps, score_used = (
            sem(n) for n in ("ad_ready", "mask_ready", "parts_ready", "partsT_ps", "partsT_sb", "ohT_ps", "ohT_sb",
                             "score_ps", "score_used"))
        c_ready, c_ps, arg_ready, w_ready, msg_ready, marg_ready, mexp_ready = (
            sem(n) for n in ("c_ready", "c_ps", "arg_ready", "w_ready", "msg_ready", "marg_ready", "mexp_ready"))
        fin_load, fin_done, s_out = [sem("fin_load0"), sem("fin_load1")], sem("fin_done"), [sem("s_out0"), sem("s_out1")]
        c_fin, merge_chain = sem("c_fin"), sem("merge_chain")

        mask = sb("mask", [P, CHUNKS, P], bf16)
        ohT = sb("ohT", [P, CHUNKS, P], bf16)
        parts = sb("parts", [P, 2, 3, 32], bf16)
        resid = sb("resid", [P, 2, 32])
        partsT = sb("partsT", [96, 2, P], bf16)
        adw = sb("adw", [P, HEADS])
        mk = sb("mk", [P, CHUNKS, HEADS])
        mg = sb("mg", [P, HEADS])
        iotab = sb("iotab", [P, P], bf16)
        cparts = sb("cparts", [P, 3, 2 * HEADS], bf16)
        cres = sb("cres", [P, 2 * HEADS])
        cbs = sb("cbs", [P, CHUNKS, 2 * HEADS])
        ca = sb("ca", [P, 2 * HEADS])
        z = sb("z", [P, CHUNKS, HEADS])
        z2 = sb("z2", [P, CHUNKS, HEADS])
        h_flat = h_res[:, :, :].rearrange("p b d -> p (b d)")
        M = h_flat[:, 0:CHUNKS * XT].rearrange("p (c k) -> p c k", c=CHUNKS)
        cc = sb("cc", [P, 6, HEADS])
        marg = sb("marg", [P, 2 * HEADS])
        mexp = sb("mexp", [P, 2 * HEADS])
        scaled = sb("scaled", [P, XT])

        tT = sb("tT", [P, 2, P])
        hid = onehot[:, :, :].rearrange("p a b -> p (a b)")[:, 0:2 * H].rearrange("p (s c n) -> p s c n", s=2, c=H // P)
        g_flat = G[:, :, :, :].rearrange("p s a b -> p (s a b)")
        A = g_flat[:, 0:2 * BATCH * D].rearrange("p (s b d) -> p s b d", s=2, d=D)
        B = g_flat[:, 2 * BATCH * D:4 * BATCH * D].rearrange("p (s b d) -> p s b d", s=2, d=D)
        xt_sbuf = g_flat[:, 4 * BATCH * D:4 * BATCH * D + 2 * (XT + HEADS)].rearrange("p (s n) -> p s n", s=2)
        fin = G[:, :, 0:BATCH, :].rearrange("p s b d -> p s (b d)")

        def slot_blocks(k):
            return (BATCH + 1 - k) // 2

        dve_stop, pe_stop, sp_stop, pool_stop, act_stop = (Stops(sem(f"{n}_stop")) for n in ("dve", "pe", "sp", "pool", "act"))

        def load_plan(eng, g):
            base = eng.value_load(plan[0:1, bass.ds(g, 1), 0:1], min_val=0, max_val=N - 1)
            windows = eng.value_load(plan[0:1, bass.ds(g, 1), 1:2], min_val=1, max_val=BLOCKS)
            passes = eng.value_load(plan[0:1, bass.ds(g, 1), 2:3], min_val=0, max_val=GROUPS * BLOCKS)
            return base, windows, passes

        def load_two(eng, i):
            passes = eng.value_load(plan[0:1, bass.ds(i * 2, 1), 2:3], min_val=0, max_val=GROUPS * BLOCKS)
            windows = [eng.value_load(plan[0:1, bass.ds(i * 2 + s, 1), 1:2], min_val=1, max_val=BLOCKS) for s in range(2)]
            return [(windows[0], passes), (windows[1], passes + windows[0])]

        block = ctx.enter_context(nc.Block())

        def store_out(sp, q):
            s = q % 2
            sp.wait_ge(fin_done, q + 1)
            lo = q * BATCH
            nb = BATCH - 1 if q == BATCHES - 1 else BATCH
            sp.dma_start(out[lo * P:(lo + nb) * P, :].rearrange("(b p) d -> p b d", p=P),
                         x_res[:, lo:lo + nb, :]).then_inc(s_out[s], 16)
            if q == BATCHES - 1:
                sp.dma_start(out[(BLOCKS - 1) * P:N, :], x_res[0:TAIL_ROWS, BLOCKS - 1, :]).then_inc(s_out[s], 16)

        @block.sync
        def _(sp):
            full = E - (E - (GROUPS - 1) * GROUP)
            sp.wait_ge(s_edges_set, 3)
            for tile, arr in ((src_all, src), (idx0_all, typ), (dst_raw, dst)):
                sp.dma_start(tile[:, 0:GROUPS - 1, :],
                             arr[0:full].rearrange("(g p c) -> p g c", p=P, c=CHUNKS)).then_inc(s_edges, 16)
                sp.dma_start(tile[0:LAST_FULL, GROUPS - 1, :],
                             arr[full:full + LAST_FULL * CHUNKS].rearrange("(p c) -> p c", c=CHUNKS)).then_inc(s_edges, 16)
                sp.dma_start(tile[LAST_FULL:LAST_FULL + 1, GROUPS - 1, 0:LAST_REST],
                             arr[full + LAST_FULL * CHUNKS:E].rearrange("(p c) -> p c", p=1)).then_inc(s_edges, 16)
            sp.wait_ge(s_pool, 9)
            sp.dma_start(agg_state[BLOCKS * P:PAD_ROWS, :], zeros[:, 0:D]).then_inc(s_agg, 16)
            for k, (lo, hi) in enumerate(((PAD_ROWS, PAD_ROWS + BATCH * P), (PAD_ROWS + BATCH * P, AGG_ROWS))):
                sp.dma_start(agg_state[lo:hi, :].rearrange("(b p) d -> p b d", p=P),
                             zeros[:, 0:D].rearrange("p (o d) -> p o d", o=1).to_broadcast([P, (hi - lo) // P, D])).then_inc(s_xt[k], 16)
            sp.dma_start(ad_table[BLOCKS * P:PAD_ROWS, :], zeros[:, 0:HEADS]).then_inc(s_store[0], 16)
            sp.dma_start(xt_table[BLOCKS * P:PAD_ROWS, :], zeros[:, 0:XT]).then_inc(s_store[1], 16)
            sp.dma_start(att_state.rearrange("(b p) c -> p b c", p=P),
                         zeros[:, :].rearrange("p (o c) -> p o c", o=1).to_broadcast([P, BLOCKS + 1, ST])).then_inc(att_stored, 16)

            with sp.Fori(0, BLOCKS // 2) as i:
                for s in range(2):
                    b = i * 2 + s
                    sp.wait_ge(xwA_sb, b + 3)
                    sp.wait_ge(xwB_sb, b + 3)
                    sp.dma_start(rel_table.rearrange("(n r) e -> n (r e)", r=R)[bass.ds(b * P, P), :],
                                 xw[:, s, 0:R * D]).then_inc(s_store[s], 16)
                    sp.dma_start(agg_state[bass.ds(b * P, P), :], xw[:, s, R * D:]).then_inc(s_store[s], 16)
            for s in range(2):
                sp.wait_ge(s_store[s], 16 + 32 * (BLOCKS // 2))
            sp.sem_inc(tables_ready[0], 1)

            with sp.Fori(0, GROUPS) as g:
                base, windows, passes = load_plan(sp, g)
                with sp.Fori(0, windows) as w:
                    t = passes + w
                    row = nc.s_assert_within(base + w * P, 0, N - 1, skip_runtime_bounds_check_because="it is at most the group's greatest destination")
                    sp.wait_ge(s_agg, (t + 1) * 16)
                    sp.dma_start(old[:, 0:D], agg_state[bass.ds(row, P), :]).then_inc(e0["old_ready"], 16)
                    sp.wait_ge(e0["merged"], t + 2)
                    sp.dma_start(agg_state[bass.ds(row, P), :], new[:, 0:D]).then_inc(s_agg, 16)
            total = sp.value_load(plan[0:1, 0:1, 3:4], min_val=1, max_val=GROUPS * BLOCKS)
            sp.wait_ge(s_agg, (total + 1) * 16)
            sp_stop(sp)

            def load_batch(q, s):
                sp.dma_start(A[:, s, :, :], agg_state[bass.ds(q * (BATCH * P), BATCH * P), :].rearrange("(b p) d -> p b d", p=P)).then_inc(a_load[s], 16)

            for s in range(2):
                load_batch(s, s)
            with sp.Fori(0, BATCHES // 2) as i:
                for s in range(2):
                    q = i * 2 + s
                    sp.wait_ge(down_ps, q * BATCH + BATCH)
                    load_batch(q + 2, s)
                    for j in range(BATCH):
                        b = q * BATCH + j
                        sp.wait_ge(xt_sb, b + 3)
                        sp.dma_start(xt_table[bass.ds(b * P, P), :], xt_sbuf[:, j % 2, 0:XT]).then_inc(s_xt[j % 2], 16)
                        sp.dma_start(ad_table[bass.ds(b * P, P), :], xt_sbuf[:, j % 2, XT:]).then_inc(s_xt[j % 2], 16)
            for k in range(2):
                sp.wait_ge(s_xt[k], 16 + 32 * BATCHES * slot_blocks(k))
                sp.wait_ge(a_load[k], 16 * (BATCHES // 2 + 1))
            sp.sem_inc(tables_ready[1], 1)

            with sp.Fori(0, GROUPS) as g:
                base, windows, passes = load_plan(sp, g)
                with sp.Fori(0, windows) as w:
                    t = passes + w
                    row = nc.s_assert_within(base + w * P, 0, N - 1, skip_runtime_bounds_check_because="it is at most the group's greatest destination")
                    sp.wait_ge(e1["merged"], t + 1)
                    sp.dma_start(adw[:, :], ad_table[bass.ds(row, P), :]).then_inc(ad_ready, 16)
                    sp.wait_ge(att_stored, (t + 1) * 16)
                    sp.dma_start(old[:, :], att_state[bass.ds(row, P), :]).then_inc(e1["old_ready"], 16)
                    sp.wait_ge(e1["merged"], t + 2)
                    sp.dma_start(att_state[bass.ds(row, P), :], new[:, :]).then_inc(att_stored, 16)
            total = sp.value_load(plan[0:1, 0:1, 3:4], min_val=1, max_val=GROUPS * BLOCKS)
            sp.wait_ge(att_stored, (total + 1) * 16)

            for q in range(BATCHES):
                s = q % 2
                if q >= 2:
                    sp.wait_ge(s_out[s], 16 * (q // 2))
                sp.dma_start(fin[:, s, 0:BATCH * XT].rearrange("p (b c) -> p b c", c=XT),
                             att_state[q * BATCH * P:(q + 1) * BATCH * P, 0:XT].rearrange("(b p) c -> p b c", p=P)).then_inc(fin_load[s], 16)
                if q >= 1:
                    store_out(sp, q - 1)
            store_out(sp, BATCHES - 1)
            for s in range(2):
                n = len([q for q in range(BATCHES) if q % 2 == s])
                sp.wait_ge(s_out[s], 16 * n + (16 if s == (BATCHES - 1) % 2 else 0))

        @block.gpsimd
        def _(pool):
            g = nc.gpsimd
            g.memset(x_res[:, BLOCKS - 1:, :], 0.0).then_inc(s_const, 1)
            g.memset(h_res[:, BLOCKS:, :], 0.0).then_inc(s_const, 1)
            g.memset(rstd_all[:, :], 0.0).then_inc(s_const, 1)
            g.memset(shift_all[:, :], 0.0).then_inc(s_const, 1)
            g.memset(src_all[:, GROUPS - 1:, :], 0).then_inc(s_edges_set, 1)
            g.memset(idx0_all[:, GROUPS - 1:, :], 0).then_inc(s_edges_set, 1)
            g.memset(dst_raw[:, GROUPS - 1:, :], -1).then_inc(s_edges_set, 1)
            g.memset(ident[:, :], 0.0).then_inc(s_pool, 1)
            g.memset(ident4[:, :, :], 0.0).then_inc(s_pool, 1)
            g.memset(pick[:, :], 0.0).then_inc(s_pool, 1)
            g.memset(upper[:, :], 1.0).then_inc(s_pool, 1)
            g.memset(a8[:, D:], 0.0).then_inc(s_pool, 1)
            g.memset(parts[:, :, :, :], 0.0).then_inc(s_pool, 1)
            g.memset(zeros[:, 0:XT], 0.0).then_inc(s_pool, 1)
            g.memset(zeros[:, XT:], -BIG).then_inc(s_pool, 1)
            g.iota(iota[:, :], pattern=[[1, P]], base=0, channel_multiplier=0,
                   allow_small_or_imprecise_dtypes=True).then_inc(s_pool, 1)
            g.iota(iotab[:, :], pattern=[[1, P]], base=0, channel_multiplier=0,
                   allow_small_or_imprecise_dtypes=True).then_inc(s_pool, 1)
            pool.wait_ge(s_pool, 10)
            g.affine_select(out=ident[:, :], in_=ident[:, :], compare_op=ALU.not_equal, fill=1.0, base=0,
                            pattern=[[-1, P]], channel_multiplier=1).then_inc(s_pool, 1)
            g.affine_select(out=ident4[:, :, :], in_=ident4[:, :, :], compare_op=ALU.not_equal, fill=1.0, base=0,
                            pattern=[[0, HEADS], [-1, P]], channel_multiplier=1).then_inc(s_pool, 1)
            for k in range(3):
                g.affine_select(out=pick[:, :], in_=pick[:, :], compare_op=ALU.not_equal, fill=1.0, base=-32 * k,
                                pattern=[[-1, 32]], channel_multiplier=1).then_inc(s_pool, 1)
                pool.wait_ge(s_pool, 13 + k)
            g.affine_select(out=upper[:, :], in_=upper[:, :], compare_op=ALU.is_gt, fill=0.0, base=0,
                            pattern=[[1, P]], channel_multiplier=-1).then_inc(s_pool, 1)

            with pool.Fori(0, BLOCKS // 2) as i:
                for s in range(2):
                    b = i * 2 + s
                    pool.wait_ge(h_ready, b + 1)
                    g.tensor_copy(h_res[:, bass.ds(b, 1), :].rearrange("p a d -> p (a d)"), hs[:, s, :]).then_inc(h_saved, 1)

            def split(gr, s, i):
                pool.wait_ge(e1["gathered"][s], i * (16 * CHUNKS) + 16 * CHUNKS)
                pool.wait_ge(partsT_ps, gr + 1)
                pool_stop(pool)
                c = Chain(pool, split_chain, gr * 6)
                for k in range(2):
                    c.beside(g.tensor_copy(parts[:, k, 0, :].rearrange("p (c h) -> p c h", h=HEADS), G[:, s, k * 8:k * 8 + 8, D:XT]))
                c.wait()
                for k in range(2):
                    c.beside(g.tensor_tensor(resid[:, k, :].rearrange("p (c h) -> p c h", h=HEADS), G[:, s, k * 8:k * 8 + 8, D:XT],
                                             parts[:, k, 0, :].rearrange("p (c h) -> p c h", h=HEADS), ALU.subtract))
                c.wait()
                pool_stop(pool)
                c.step(g.tensor_copy(parts[:, :, 1, :], resid[:, :, :]))
                c.step(g.tensor_tensor(resid[:, :, :], resid[:, :, :], parts[:, :, 1, :], ALU.subtract))
                pool_stop(pool)
                g.tensor_copy(parts[:, :, 2, :], resid[:, :, :]).then_inc(parts_ready, 1)
                assert c.n == 6

            def gathers(sems, table, width, ready):
                pool.wait_ge(ready, 1)
                with pool.Fori(0, GROUPS // 2) as i:
                    for s in range(2):
                        gr = i * 2 + s
                        pool.wait_ge(sems["idx_ready"], gr + 1)
                        pool.wait_ge(sems["group_free"], gr + 1)
                        pool_stop(pool)
                        for c in range(CHUNKS):
                            g.indirect_dma_start(out=G[:, s, c, 0:width], out_offset=None, in_=table,
                                                 in_offset=bass.IndirectOffsetOnAxis(ap=idx[:, s, c:c + 1], axis=0)).then_inc(sems["gathered"][s], 16)
                        if sems is e1:
                            split(gr, s, i)

            gathers(e0, rel_table, D, tables_ready[0])

            def residuals(q, s):
                pool.wait_ge(norm1_done, q * BATCH + BATCH)
                pool_stop(pool)
                g.tensor_tensor(A[:, s, :, :], A[:, s, :, :], rows[:, 1:2, :].to_broadcast([P, BATCH, D]), ALU.mult).then_inc(affine_half, 1)
                pool.wait_ge(affine_half, q + 1)
                g.tensor_tensor(A[:, s, :, :], A[:, s, :, :], rows[:, 2:3, :].to_broadcast([P, BATCH, D]), ALU.add).then_inc(affine_done, 1)
                pool.wait_ge(gelu_done, q + 1)
                pool_stop(pool)
                hb = h_res[:, bass.ds(q * BATCH, BATCH), :]
                xb = x_res[:, bass.ds(q * BATCH, BATCH), :]
                g.tensor_tensor(hb, hb, B[:, s, :, :], ALU.add).then_inc(hadd_done, 1)
                pool.wait_ge(hadd_done, q + 1)
                pool_stop(pool)
                g.tensor_tensor(xb, xb, hb, ALU.add).then_inc(xadd_done, 1)

            residuals(0, 0)
            with pool.Fori(0, BATCHES // 2) as i:
                for s in range(2):
                    residuals(i * 2 + s + 1, 1 - s)
            gathers(e1, xt_table, XT, tables_ready[1])

        @block.scalar
        def _(act):
            a = nc.scalar
            act.wait_ge(s_const, 4)
            for q in range(BATCHES):
                lo, hi = q * BATCH, min((q + 1) * BATCH, BLOCKS - 1)
                act.dma_start(x_res[:, lo:hi, :], x[lo * P:hi * P, :].rearrange("(b p) d -> p b d", p=P)).then_inc(s_x, 16)
            act.dma_start(x_res[0:TAIL_ROWS, BLOCKS - 1, :], x[(BLOCKS - 1) * P:N, :]).then_inc(s_x, 16)
            act.dma_start(w_all[:, 0:R * D].rearrange("p (r e) -> p r e", r=R), W_rel.rearrange("r d e -> d r e")).then_inc(s_load, 16)
            act.dma_start(w_all[:, R * D:], W_self).then_inc(s_load, 16)
            act.dma_start(w1[:, :], W1).then_inc(s_load, 16)
            act.dma_start(w2[:, :, :], W2.rearrange("(c p) d -> p c d", p=P)).then_inc(s_load, 16)
            act.dma_start(linw[:, :, :], lin_w.rearrange("b o i -> o b i")).then_inc(s_load, 16)
            for k, v in enumerate((b_conv, g1, b1n, b2)):
                act.dma_start(rows[:, k, :], v.rearrange("(o d) -> o d", o=1).to_broadcast([P, D])).then_inc(s_load, 16)
            act.dma_start(coef[:, :], coeffs.rearrange("(o d) -> o d", o=1).to_broadcast([P, 3])).then_inc(s_load, 16)
            with nc.allow_non_contiguous_dma("small columns"):
                act.dma_start(cols[:, 0:1], g2.rearrange("(p o) -> p o", o=1)).then_inc(s_load, 16)
                act.dma_start(cols[:, 1:2], b2n.rearrange("(p o) -> p o", o=1)).then_inc(s_load, 16)
                act.dma_start(b1col[:, :], b1.rearrange("(c p) -> p c", p=P)).then_inc(s_load, 16)
                act.dma_start(linb[:, :], lin_b.rearrange("b o -> o b")).then_inc(s_load, 16)
                act.dma_start(atts[:, 0, :], att_src.rearrange("b q h c -> (q h c) b")).then_inc(s_load, 16)
                act.dma_start(atts[:, 1, :], att_dst.rearrange("b q h c -> (q h c) b")).then_inc(s_load, 16)

            act.sem_inc(xwB_sb, 2)

            def norm(b, s):
                a.activation(hs[:, s, :], x_res[:, bass.ds(b, 1), :].rearrange("p a d -> p (a d)"), ACT.Relu,
                             bias=shift_all[:, bass.ds(b, 1)], scale=rstd_all[:, bass.ds(b, 1)]).then_inc(h_ready, 1)

            act.wait_ge(h_norm, BATCHES)
            for s in range(2):
                norm(s, s)
            with act.Fori(0, BLOCKS // 2) as i:
                for s in range(2):
                    b = i * 2 + s
                    act.wait_ge(xw_ps, b + 1)
                    act.wait_ge(s_store[s], i * 32 + 16)
                    a.copy(xw[:, s, 512:R * D], banks[2 + 3 * s][:, :]).then_inc(xwB_sb, 1)
                    act.wait_ge(h_saved, b + 1)
                    norm(b + 2, s)

            def indices(sems, all_idx):
                for s in range(2):
                    a.copy(idx[:, s, :], all_idx[:, s, :]).then_inc(sems["idx_ready"], 1)

            def next_indices(sems, all_idx, i, s):
                act.wait_ge(sems["gathered"][s], i * (16 * CHUNKS) + 16 * CHUNKS)
                a.copy(idx[:, s, :], all_idx[:, bass.ds(i * 2 + (s + 2), 1), :].rearrange("p a c -> p (a c)")).then_inc(sems["idx_ready"], 1)

            act.wait_ge(s_plan, 1)
            indices(e0, idx0_all)
            with act.Fori(0, GROUPS // 2) as i:
                for s in range(2):
                    next_indices(e0, idx0_all, i, s)
            act.wait_ge(e0["idx_ready"], GROUPS + 2)

            def norm_rows(q, out_tile, in_rows, k, func, done):
                act.wait_ge(n_ready[k], q + 1)
                act_stop(act)
                for j in range(BATCH):
                    a.activation(out_tile[:, j, :], in_rows(j), func, bias=shift3[k][:, j:j + 1], scale=rstd3[k][:, j:j + 1]).then_inc(done, 1)

            def row_of(tile, q):
                return lambda j: tile[:, bass.ds(q * BATCH + j, 1), :].rearrange("p a d -> p (a d)")

            def first_norm(q, s):
                norm_rows(q, A[:, s, :, :], lambda j: A[:, s, j, :], 0, ACT.Identity, norm1_done)

            def second_norm(q, s):
                act.wait_ge(affine_done, q + 1)
                a.activation(B[:, s, :, :], A[:, s, :, :], ACT.Gelu).then_inc(gelu_done, 1)
                norm_rows(q, A[:, s, :, :], row_of(h_res, q), 1, ACT.Identity, norm2_done)

            def transposed(n, j):
                act.wait_ge(t_ps, n + j + 1)
                a.copy(tT[:, j % 2, :], banks[5 * (j % 2)][:, 0:P]).then_inc(t_sb, 1)

            first_norm(0, 0)
            second_norm(0, 0)
            with act.Fori(0, BATCHES // 2) as i:
                for s in range(2):
                    q = i * 2 + s
                    transposed(q * (2 * BATCH), 0)
                    for j in range(BATCH):
                        if j + 1 < BATCH:
                            transposed(q * (2 * BATCH), j + 1)
                        act.wait_ge(up_ps, q * BATCH + j + 1)
                        for c in range(H // P):
                            a.activation(hid[:, j % 2, c, :], banks[1 + j % 2][:, c * P:(c + 1) * P], ACT.Gelu, bias=b1col[:, c:c + 1]).then_inc(up_sb, 1)
                        if j == 2:
                            first_norm(q + 1, 1 - s)
                    second_norm(q + 1, 1 - s)
                    norm_rows(q, B[:, s, :, :], row_of(x_res, q), 2, ACT.Relu, norm3_done)
                    for j in range(BATCH):
                        transposed(q * (2 * BATCH) + BATCH, j)

            act.sem_inc(e1["oh_ready"], 1)
            act.sem_inc(mexp_ready, 1)
            indices(e1, src_all)
            with act.Fori(0, GROUPS // 2) as i:
                plans = load_two(act, i)
                for s in range(2):
                    g = i * 2 + s
                    windows, passes = plans[s]
                    act.wait_ge(partsT_ps, g + 2)
                    a.copy(partsT[:, :, :].rearrange("p a b -> p (a b)"), banks[6][0:96, 0:128].bitcast(bf16)).then_inc(partsT_sb, 1)
                    with act.Fori(0, windows) as w:
                        t = passes + w
                        act.wait_ge(mask_ready, (t + 1) * CHUNKS)
                        act.wait_ge(e1["agg_done"], t + 1)
                        a.activation(onehot[:, :, :], mask[:, :, :], ACT.Copy, bias=1.0, scale=1.0 / BIG).then_inc(e1["oh_ready"], 1)
                        for half in range(2):
                            act.wait_ge(ohT_ps, t * 2 + half + 1)
                            a.activation(ohT[:, half * 8:half * 8 + 8, :].rearrange("p c e -> p (c e)"), banks[4 + half][:, :].bitcast(bf16),
                                         ACT.Copy, bias=1.0, scale=1.0 / BIG).then_inc(ohT_sb, 1)
                        act.wait_ge(marg_ready, t + 1)
                        a.activation(mexp[:, :], marg[:, :], ACT.Exp).then_inc(mexp_ready, 1)
                        act.wait_ge(arg_ready, t + 1)
                        a.activation(M[:, :, D:XT], z[:, :, :], ACT.Exp).then_inc(w_ready, 1)
                    next_indices(e1, src_all, i, s)

        @block.vector
        def _(dve):
            v = nc.vector
            ch = Chain(dve, c_dve)
            dve.wait_ge(s_edges, 16 * 9)
            ch.step(v.scalar_tensor_tensor(idx0_all[:, 0:GROUPS, :], src_all[:, 0:GROUPS, :], float(R), idx0_all[:, 0:GROUPS, :], ALU.mult, ALU.add))
            ch.step(v.tensor_copy(dst_all[:, :, :], dst_raw[:, :, :]))
            ch.step(v.tensor_reduce(span[:, 1, :], dst_all[:, :, :], AX.X, ALU.max))
            pad = h_res[:, 0:13, :].rearrange("p a b -> p (a b)")[:, 0:GROUPS * CHUNKS].rearrange("p (g c) -> p g c", c=CHUNKS)
            ch.step(v.tensor_scalar(pad, dst_all[:, :, :], 0.0, float(1 << 20), ALU.is_lt, ALU.mult))
            ch.step(v.tensor_tensor(pad, pad, dst_all[:, :, :], ALU.add))
            ch.step(v.tensor_reduce(span[:, 0, :], pad, AX.X, ALU.min))
            dve.sem_inc(s_setdve, 1)
            dve.wait_ge(s_setpe, 1)
            ch.step(v.tensor_reduce(spanc[:, 0:1], banks[0][0:GROUPS, 0:P], AX.X, ALU.min))
            ch.step(v.tensor_reduce(spanc[:, 1:2], banks[0][0:GROUPS, P:2 * P], AX.X, ALU.max))
            ch.step(v.tensor_tensor(spani[:, :], spanc[:, 1:2], spanc[:, 0:1], ALU.subtract))
            ch.step(v.tensor_scalar(spani[:, :], spani[:, :], 7, None, ALU.arith_shift_right))
            ch.step(v.tensor_scalar(spanc[:, 2:3], spani[:, :], 1.0, None, ALU.add))
            dve.sem_inc(s_setdve, 1)
            dve.wait_ge(s_setpe, 2)
            ch.step(v.tensor_copy(base_all[:, :], banks[1][:, 0:GROUPS]))
            for k in range(3):
                ch.step(v.tensor_copy(plan[:, :, k], banks[1][0:1, k * GROUPS:(k + 1) * GROUPS]))
            ch.step(v.tensor_copy(tmp[0:1, 0:1], banks[1][0:1, 2 * GROUPS - 1:2 * GROUPS]))
            ch.step(v.tensor_tensor(plan[:, 0, 3:4], tmp[0:1, 0:1], banks[1][0:1, 3 * GROUPS - 1:3 * GROUPS], ALU.add))
            dve.sem_inc(s_plan, 1)

            dve.wait_ge(s_load, 16 * 16)
            dve.wait_ge(s_pool, 16)
            for dstt, srct in ((wcomb[:, :], [linw[:, k, :] for k in range(3)]), (bcomb[:, :], [linb[:, k:k + 1] for k in range(3)]),
                               (acomb[:, 0:1], [atts[:, 0, k:k + 1] for k in range(3)]), (acomb[:, 1:2], [atts[:, 1, k:k + 1] for k in range(3)])):
                ch.step(v.tensor_scalar(dstt, srct[0], coef[:, 0:1], None, ALU.mult))
                for k in (1, 2):
                    ch.step(v.scalar_tensor_tensor(dstt, srct[k], coef[:, k:k + 1], dstt, ALU.mult, ALU.add))
            ch.step(v.tensor_copy(a8[:, 0:D], ident[:, :]))
            for k in range(2):
                for hd in range(HEADS):
                    ch.step(v.tensor_copy(a8[hd * HC:(hd + 1) * HC, D + k * HEADS + hd:D + k * HEADS + hd + 1],
                                          acomb[hd * HC:(hd + 1) * HC, k:k + 1]))
            dve.sem_inc(s_setdve, 1)
            dve.wait_ge(s_setpe, 3)
            ch.step(v.tensor_copy(wx[:, :], banks[0][:, 0:XT + HEADS]))
            ch.step(v.tensor_copy(bx[:, :], banks[1][:, 0:XT + HEADS]))
            ch.step(v.tensor_tensor(b1col[:, :], b1col[:, :], banks[2][:, 0:H // P], ALU.add))
            ch.step(v.tensor_scalar(w1[:, :], w1[:, :], cols[:, 0:1], None, ALU.mult))
            dve.sem_inc(s_setdve, 1)

            n0 = ch.n
            dve.wait_ge(s_x, 16 * (BATCHES + 1))
            dve.wait_ge(s_const, 4)
            with dve.Fori(0, BATCHES) as q:
                c = Chain(dve, c_dve, q * STATS_STEPS + n0)
                stats_steps(nc, c, dve_stop, [x_res[:, bass.ds(q * BATCH + j, 1), :].rearrange("p a d -> p (a d)") for j in range(BATCH)],
                            stats, mv, None, var[:, :], tmp[:, :], rstd_all[:, bass.ds(q * BATCH, BATCH)], shift_all[:, bass.ds(q * BATCH, BATCH)])
                dve.sem_inc(h_norm, 1)
            assert c.n == STATS_STEPS, c.n

            dve.sem_inc(xwA_sb, 2)
            with dve.Fori(0, BLOCKS // 2) as i:
                for s in range(2):
                    b = i * 2 + s
                    dve.wait_ge(hT_ps, b + 1)
                    v.tensor_copy(hT[:, s, :], banks[0][:, s * P:(s + 1) * P]).then_inc(hT_sb, 1)
                    dve.wait_ge(xw_ps, b + 1)
                    dve.wait_ge(s_store[s], i * 32 + 16)
                    v.tensor_tensor(xw[:, s, R * D:], banks[3 + 3 * s][:, 0:D], rows[:, 0, :], ALU.add)
                    v.tensor_copy(xw[:, s, 0:512], banks[1 + 3 * s][:, :]).then_inc(xwA_sb, 1)

            def window(sems, c, g):
                c.step(v.tensor_scalar(rel[:, :], rel[:, :], -float(P), None, ALU.add))
                for k in range(CHUNKS):
                    ins = v.tensor_scalar(onehot[:, k, :], iota[:, :], rel[:, k:k + 1], None, ALU.is_equal)
                ins.then_inc(sems["oh_ready"], 1)

            def mask_window(sems, c):
                c.step(v.tensor_scalar(rel[:, :], rel[:, :], -float(P), None, ALU.add))
                for k in range(CHUNKS):
                    v.tensor_scalar(mask[:, k, :], iotab[:, :], rel[:, k:k + 1], -BIG, ALU.not_equal, ALU.mult).then_inc(mask_ready, 1)

            def first_rel(sems, g):
                v.tensor_scalar(rel[:, :], dst_all[:, bass.ds(g, 1), :].rearrange("p a c -> p (a c)"),
                                base_all[:, bass.ds(g, 1)], float(P), ALU.subtract, ALU.add).then_inc(sems["chain"], 1)

            dve.sem_inc(e0["merged"], 1)
            with dve.Fori(0, GROUPS) as g:
                base, windows, passes = load_plan(dve, g)
                first_rel(e0, g)
                dve.wait_ge(e0["chain"], passes + g + 1)
                dve_stop(dve)
                with dve.Fori(0, windows) as w:
                    t = passes + w
                    window(e0, Chain(dve, e0["chain"], t + g + 1), g)
                    dve.wait_ge(e0["agg_done"], t + 1)
                    dve.wait_ge(e0["old_ready"], (t + 1) * 16)
                    v.tensor_tensor(new[:, 0:D], banks[7][:, 0:D], old[:, 0:D], ALU.add).then_inc(e0["merged"], 1)

            def norm_stats(c, q, k, row):
                stats_steps(nc, c, dve_stop, [row(j) for j in range(BATCH)], stats, mv, None, var[:, :], tmp[:, :], rstd3[k][:, :], shift3[k][:, :])
                dve.sem_inc(n_ready[k], 1)

            def first_stats(c, q, s, i):
                dve.wait_ge(a_load[s], i * 16 + 16)
                norm_stats(c, q, 0, lambda j: A[:, s, j, :])

            def second_stats(c, q):
                dve.wait_ge(hadd_done, q + 1)
                norm_stats(c, q, 1, lambda j: h_res[:, bass.ds(q * BATCH + j, 1), :].rearrange("p a d -> p (a d)"))

            dve.sem_inc(ff_ready, 2)
            dve.sem_inc(xt_sb, 2)
            c = Chain(dve, c_dense)
            first_stats(c, 0, 0, 0)
            second_stats(c, 0)
            n0, DENSE = c.n, STATS_STEPS * 3 + 1
            with dve.Fori(0, BATCHES // 2) as i:
                for s in range(2):
                    q = i * 2 + s
                    c = Chain(dve, c_dense, q * DENSE + n0)
                    xb = x_res[:, bass.ds(q * BATCH, BATCH), :]
                    first_stats(c, q + 1, 1 - s, i + s)
                    for j in range(BATCH):
                        dve.wait_ge(down_ps, q * BATCH + j + 1)
                        v.tensor_tensor(B[:, s, j, :], banks[3 + 3 * (j % 2)][:, 0:P], rows[:, 3, :], ALU.add).then_inc(ff_ready, 1)
                    second_stats(c, q + 1)
                    dve.wait_ge(xadd_done, q + 1)
                    dve.wait_ge(ff_ready, q * BATCH + BATCH + 2)
                    c.step(v.tensor_tensor(xb, xb, B[:, s, :, :], ALU.add))
                    norm_stats(c, q, 2, lambda j: x_res[:, bass.ds(q * BATCH + j, 1), :].rearrange("p a d -> p (a d)"))
                    assert c.n == DENSE, c.n
                    for j in range(BATCH):
                        dve.wait_ge(xt_ps, q * BATCH + j + 1)
                        dve.wait_ge(s_xt[j % 2], q * (32 * slot_blocks(j % 2)) + (16 + 32 * (j // 2)))
                        v.tensor_tensor(xt_sbuf[:, j % 2, :], banks[4 + 3 * (j % 2)][:, 0:XT + HEADS], bx[:, :], ALU.add).then_inc(xt_sb, 1)

            dve.wait_ge(xt_sb, BLOCKS + 2)
            for tile in (old[:, :], new[:, :], mexp[:, :], onehot[:, :, :]):
                v.memset(tile, 0.0).then_inc(merge_chain, 1)
            dve.wait_ge(merge_chain, 4)
            v.memset(M[:, :, :], 0.0).then_inc(msg_ready, 3)

            def merge(t):
                c = Chain(dve, merge_chain, t * 4 + 4)
                dve.wait_ge(mexp_ready, t + 1)
                c.step(v.tensor_tensor(scaled[:, 0:D].rearrange("p (h k) -> p h k", h=HEADS), old[:, 0:D].rearrange("p (h k) -> p h k", h=HEADS),
                                       mexp[:, 0:HEADS].rearrange("p (h o) -> p h o", o=1).to_broadcast([P, HEADS, HC]), ALU.mult))
                c.step(v.tensor_tensor(scaled[:, D:XT], old[:, D:XT], mexp[:, 0:HEADS], ALU.mult))
                dve.wait_ge(e1["agg_done"], t + 1)
                c.step(v.tensor_tensor(new[:, 0:D].rearrange("p (h k) -> p h k", h=HEADS), banks[7][:, 0:D].rearrange("p (h k) -> p h k", h=HEADS),
                                       mexp[:, HEADS:].rearrange("p (h o) -> p h o", o=1).to_broadcast([P, HEADS, HC]), ALU.mult))
                c.step(v.tensor_tensor(new[:, D:XT], banks[7][:, D:XT], mexp[:, HEADS:], ALU.mult))
                v.tensor_tensor(new[:, 0:XT], new[:, 0:XT], scaled[:, :], ALU.add).then_inc(e1["merged"], 1)

            PSTEPS = 19
            with dve.Fori(0, GROUPS // 2) as i:
                plans = load_two(dve, i)
                for s in range(2):
                    g = i * 2 + s
                    windows, passes = plans[s]
                    c = Chain(dve, e1["chain"], passes * PSTEPS + g)
                    c.step(v.tensor_scalar(rel[:, :], dst_all[:, bass.ds(g, 1), :].rearrange("p a c -> p (a c)"),
                                           base_all[:, bass.ds(g, 1)], float(P), ALU.subtract, ALU.add))
                    dve_stop(dve)
                    with dve.Fori(0, windows) as w:
                        t = passes + w
                        c = Chain(dve, e1["chain"], t * PSTEPS + g + 1)
                        dve.wait_ge(e1["oh_ready"], t + 1)
                        mask_window(e1, c)
                        merge(t)
                        for k in range(CHUNKS // 2):
                            if k == CHUNKS // 2 - 2:
                                dve.wait_ge(ad_ready, (t + 1) * 16)
                                dve.wait_ge(e1["old_ready"], (t + 1) * 16)
                                c.beside(v.tensor_tensor(cc[:, 3, :], old[:, XT:], adw[:, :], ALU.add))
                                c.beside(v.tensor_copy(ca[:, HEADS:], adw[:, :]))
                            dve.wait_ge(score_ps, t * (CHUNKS // 2) + k + 1)
                            v.tensor_reduce(mk[:, 2 * k:2 * k + 2, :], score[k % 2], AX.X, ALU.max).then_inc(score_used, 1)
                        dve.wait_ge(score_used, t * (CHUNKS // 2) + CHUNKS // 2 + 2)
                        c.step(v.tensor_reduce(mg[:, :], mk[:, :, :].rearrange("p c h -> p h c"), AX.X, ALU.max))
                        c.beside(v.tensor_tensor(cc[:, 0, :], mg[:, :], adw[:, :], ALU.add))
                        c.step(v.tensor_tensor(new[:, XT:], old[:, XT:], mg[:, :], ALU.max))
                        c.beside(v.scalar_tensor_tensor(ca[:, 0:HEADS], cc[:, 0, :], 0.2, cc[:, 0, :], ALU.mult, ALU.max))
                        c.step(v.tensor_tensor(cc[:, 1, :], new[:, XT:], adw[:, :], ALU.add))
                        c.beside(v.tensor_copy(cparts[:, 0, :], ca[:, :]))
                        c.beside(v.scalar_tensor_tensor(cc[:, 4, :], cc[:, 3, :], 0.2, cc[:, 3, :], ALU.mult, ALU.max))
                        c.step(v.scalar_tensor_tensor(cc[:, 2, :], cc[:, 1, :], 0.2, cc[:, 1, :], ALU.mult, ALU.max))
                        c.beside(v.tensor_tensor(cres[:, :], ca[:, :], cparts[:, 0, :], ALU.subtract))
                        c.step(v.tensor_tensor(marg[:, 0:HEADS], cc[:, 4, :], cc[:, 2, :], ALU.subtract))
                        c.beside(v.tensor_copy(cparts[:, 1, :], cres[:, :]))
                        v.tensor_tensor(marg[:, HEADS:], ca[:, 0:HEADS], cc[:, 2, :], ALU.subtract).then_inc(marg_ready, 1)
                        c.wait()
                        c.step(v.tensor_tensor(cres[:, :], cres[:, :], cparts[:, 1, :], ALU.subtract))
                        v.tensor_copy(cparts[:, 2, :], cres[:, :]).then_inc(c_ready, 1)
                        dve.wait_ge(c_ps, t + 1)
                        cb = cbs[:, :, :]
                        c.step(v.tensor_reduce(cb, banks[6][:, 128:128 + CHUNKS * 24].rearrange("p (c k j) -> p c j k", k=3, j=8), AX.X, ALU.add))
                        c.step(v.tensor_tensor(z[:, :, :], cb[:, :, HEADS:], G[:, s, :, D:XT], ALU.add))
                        c.step(v.scalar_tensor_tensor(z2[:, :, :], z[:, :, :], 0.2, z[:, :, :], ALU.mult, ALU.max))
                        c.step(v.tensor_tensor(z2[:, :, :], z2[:, :, :], cb[:, :, 0:HEADS], ALU.subtract))
                        v.tensor_scalar(z[:, :, :], z2[:, :, :], 0.0, None, ALU.min).then_inc(arg_ready, 1)
                        dve.wait_ge(w_ready, t + 1)
                        for lo, hi in zip(SLICES, SLICES[1:]):
                            v.tensor_tensor(M[:, lo:hi, 0:D].rearrange("p c (h k) -> p c h k", h=HEADS),
                                            G[:, s, lo:hi, 0:D].rearrange("p c (h k) -> p c h k", h=HEADS),
                                            M[:, lo:hi, D:XT].rearrange("p c (h o) -> p c h o", o=1).to_broadcast([P, hi - lo, HEADS, HC]),
                                            ALU.mult).then_inc(msg_ready, 1)
                        assert c.n == PSTEPS, c.n
                    dve.wait_ge(msg_ready, (passes + windows) * 3 + 3)
                    dve.sem_inc(e1["group_free"], 1)
            merge(dve.value_load(plan[0:1, 0:1, 3:4], min_val=1, max_val=GROUPS * BLOCKS))

            ch = Chain(dve, c_fin)
            for q in range(BATCHES):
                s = q % 2
                lo = q * BATCH
                f = fin[:, s, 0:BATCH * XT].rearrange("p (b c) -> p b c", c=XT)
                dve.wait_ge(fin_load[s], 16 * (q // 2 + 1))
                ch.step(v.tensor_scalar(f[:, :, D:XT], f[:, :, D:XT], 1e-16, None, ALU.add))
                ch.step(v.reciprocal(f[:, :, D:XT], f[:, :, D:XT]))
                ch.step(v.tensor_tensor(f[:, :, 0:D].rearrange("p b (h k) -> p b h k", h=HEADS), f[:, :, 0:D].rearrange("p b (h k) -> p b h k", h=HEADS),
                                        f[:, :, D:XT].rearrange("p b (h o) -> p b h o", o=1).to_broadcast([P, BATCH, HEADS, HC]), ALU.mult))
                v.tensor_tensor(x_res[:, lo:lo + BATCH, :], x_res[:, lo:lo + BATCH, :], f[:, :, 0:D], ALU.add).then_inc(fin_done, 1)

        @block.tensor
        def _(pe):
            t = nc.tensor
            pe.wait_ge(s_pool, 16)
            pe.wait_ge(s_setdve, 1)
            t.transpose(banks[0][0:GROUPS, 0:P], span[:, 0, :], ident[:, :])
            t.transpose(banks[0][0:GROUPS, P:2 * P], span[:, 1, :], ident[:, :]).then_inc(s_setpe, 1)
            pe.wait_ge(s_setdve, 2)
            t.matmul(banks[1][:, 0:GROUPS], spanc[:, 0:1].to_broadcast([GROUPS, P]), ident[0:GROUPS, 0:GROUPS], start=True, stop=True)
            t.matmul(banks[1][:, GROUPS:2 * GROUPS], spanc[:, 2:3].to_broadcast([GROUPS, P]), ident[0:GROUPS, 0:GROUPS], start=True, stop=True)
            t.matmul(banks[1][:, 2 * GROUPS:3 * GROUPS], spanc[:, 2:3].to_broadcast([GROUPS, P]), upper[0:GROUPS, 0:GROUPS], start=True, stop=True).then_inc(s_setpe, 1)
            pe.wait_ge(s_setdve, 3)
            t.matmul(banks[0][:, 0:XT + HEADS], wcomb[:, :], a8[:, :], start=True, stop=True)
            t.matmul(banks[1][:, 0:XT + HEADS], bcomb[:, 0:1].to_broadcast([P, P]), a8[:, :], start=True, stop=True)
            for c in range(H // P):
                ins = t.matmul(banks[2][:, c:c + 1], w1[:, c * P:(c + 1) * P], cols[:, 1:2], start=True, stop=True)
            ins.then_inc(s_setpe, 1)
            pe.wait_ge(s_setdve, 4)

            with pe.Fori(0, BLOCKS // 2) as i:
                for s in range(2):
                    b = i * 2 + s
                    pe.wait_ge(h_ready, b + 1)
                    pe.wait_ge(xwA_sb, b + 1)
                    pe.wait_ge(xwB_sb, b + 1)
                    t.transpose(banks[0][:, s * P:(s + 1) * P], hs[:, s, :], ident[:, :]).then_inc(hT_ps, 1)
                    pe.wait_ge(hT_sb, b + 1)
                    t.matmul(banks[1 + 3 * s][:, :], hT[:, s, :], w_all[:, 0:512], start=True, stop=True)
                    t.matmul(banks[2 + 3 * s][:, :], hT[:, s, :], w_all[:, 512:1024], start=True, stop=True)
                    t.matmul(banks[3 + 3 * s][:, 0:D], hT[:, s, :], w_all[:, R * D:], start=True, stop=True).then_inc(xw_ps, 1)

            pe.sem_inc(e0["group_free"], 2)
            with pe.Fori(0, GROUPS // 2) as i:
                for s in range(2):
                    g = i * 2 + s
                    base, windows, passes = load_plan(pe, g)
                    pe.wait_ge(e0["gathered"][s], i * (16 * CHUNKS) + 16 * CHUNKS)
                    pe_stop(pe)
                    with pe.Fori(0, windows) as w:
                        tt = passes + w
                        pe.wait_ge(e0["oh_ready"], tt + 1)
                        pe.wait_ge(e0["merged"], tt + 1)
                        for k in range(CHUNKS):
                            ins = t.matmul(banks[7][:, 0:D], onehot[:, k, :], G[:, s, k, 0:D], start=(k == 0), stop=(k == CHUNKS - 1))
                        ins.then_inc(e0["agg_done"], 1)
                    pe.wait_ge(e0["agg_done"], passes + windows)
                    pe.sem_inc(e0["group_free"], 1)

            def flip(tile, j):
                t.transpose(banks[5 * (j % 2)][:, 0:P], tile, ident[:, :]).then_inc(t_ps, 1)

            def up(q, j):
                pe.wait_ge(t_sb, q * (2 * BATCH) + j + 1)
                for c in range(H // P):
                    ins = t.matmul(banks[1 + j % 2][:, c * P:(c + 1) * P], w1[:, c * P:(c + 1) * P], tT[:, j % 2, :], start=True, stop=True)
                ins.then_inc(up_ps, 1)

            with pe.Fori(0, BATCHES // 2) as i:
                for s in range(2):
                    q = i * 2 + s
                    pe.wait_ge(norm2_done, q * BATCH + BATCH)
                    flip(A[:, s, 0, :], 0)
                    up(q, 0)
                    for j in range(BATCH):
                        if j + 1 < BATCH:
                            flip(A[:, s, j + 1, :], j + 1)
                            up(q, j + 1)
                        pe.wait_ge(up_sb, q * (BATCH * H // P) + (j + 1) * (H // P))
                        pe.wait_ge(ff_ready, q * BATCH + j + (1 if j else 2))
                        for c in range(H // P):
                            ins = t.matmul(banks[3 + 3 * (j % 2)][:, 0:P], hid[:, j % 2, c, :], w2[:, c, :], start=(c == 0), stop=(c == H // P - 1))
                        ins.then_inc(down_ps, 1)
                    pe.wait_ge(norm3_done, q * BATCH + BATCH)
                    flip(B[:, s, 0, :], 0)
                    for j in range(BATCH):
                        if j + 1 < BATCH:
                            flip(B[:, s, j + 1, :], j + 1)
                        pe.wait_ge(t_sb, q * (2 * BATCH) + (BATCH + j + 1))
                        pe.wait_ge(xt_sb, q * BATCH + j + (1 if j else 2))
                        t.matmul(banks[4 + 3 * (j % 2)][:, 0:XT + HEADS], tT[:, j % 2, :], wx[:, :], start=True, stop=True).then_inc(xt_ps, 1)

            def aggregate(tt):
                pe.wait_ge(e1["oh_ready"], tt + 1)
                for k in range(CHUNKS):
                    if k in SLICES[:-1]:
                        pe.wait_ge(msg_ready, tt * 3 + SLICES.index(k) + 1)
                    ins = t.matmul(banks[7][:, 0:XT], onehot[:, k, :], M[:, k, :], start=(k == 0), stop=(k == CHUNKS - 1))
                ins.then_inc(e1["agg_done"], 1)

            pe.sem_inc(e1["group_free"], 2)
            pe.sem_inc(score_used, 2)
            pe.sem_inc(partsT_ps, 1)
            with pe.Fori(0, GROUPS // 2) as i:
                plans = load_two(pe, i)
                for s in range(2):
                    g = i * 2 + s
                    windows, passes = plans[s]
                    pe.wait_ge(parts_ready, g + 1)
                    pe.wait_ge(msg_ready, passes * 3 + 1)
                    for half in range(2):
                        ins = t.transpose(banks[6][0:96, half * 64:half * 64 + 64].bitcast(bf16), parts[:, half, :, :].rearrange("p a b -> p (a b)"), ident4[:, 0, :])
                    ins.then_inc(partsT_ps, 1)
                    pe_stop(pe)
                    with pe.Fori(0, windows) as w:
                        tt = passes + w
                        aggregate(tt)
                        pe.wait_ge(partsT_sb, g + 1)
                        for kp in range(CHUNKS // 2):
                            pe.wait_ge(mask_ready, tt * CHUNKS + 2 * kp + 2)
                            pe.wait_ge(score_used, tt * (CHUNKS // 2) + kp + 1)
                            for k in (2 * kp, 2 * kp + 1):
                                half, kk = divmod(k, 8)
                                dstp = score[kp % 2][:, k % 2, :, :]
                                for hd in range(HEADS):
                                    q = kk * HEADS + hd
                                    t.matmul(dstp[:, hd, :], pick[:, q:q + 1].to_broadcast([96, P]), partsT[:, half, :],
                                             start=(hd == 0), stop=False)
                                ins = t.matmul(dstp, mask[:, k, :], ident4[:, :, :], start=False, stop=True)
                            ins.then_inc(score_ps, 1)
                        for half in range(2):
                            for k in range(8):
                                ins = t.transpose(banks[4 + half][:, k * 64:k * 64 + 64].bitcast(bf16), mask[:, half * 8 + k, :], ident4[:, 0, :])
                            ins.then_inc(ohT_ps, 1)
                        pe.wait_ge(ohT_sb, tt * 2 + 2)
                        pe.wait_ge(c_ready, tt + 1)
                        for k in range(CHUNKS):
                            ins = t.matmul(banks[6][:, 128 + k * 24:152 + k * 24], ohT[:, k, :], cparts[:, :, :].rearrange("p a b -> p (a b)"), start=True, stop=True)
                        ins.then_inc(c_ps, 1)
            aggregate(pe.value_load(plan[0:1, 0:1, 3:4], min_val=1, max_val=GROUPS * BLOCKS))


_INS = ["x", "src", "dst", "edge_type_8", "L0_gnn_W_rel", "L0_gnn_W_self", "L0_gnn_b_conv", "L0_gnn_ln1_g", "L0_gnn_ln1_b",
        "L0_gnn_ln2_g", "L0_gnn_ln2_b", "L0_gnn_W1", "L0_gnn_b1", "L0_gnn_W2", "L0_gnn_b2", "L1_gnn_coeffs_t",
        "L1_gnn_lin_weight", "L1_gnn_lin_bias", "L1_gnn_att_src", "L1_gnn_att_dst"]


def kernel(**inputs):
    import numpy as _np
    import concourse.bacc as _bacc
    from concourse import mybir as _mybir
    from concourse.bass_utils import run_bass_kernel_spmd as _run

    nc = _bacc.Bacc("TRN2", target_bir_lowering=False, num_devices=1)
    arrays, args = {}, []
    for name in _INS:
        a = _np.ascontiguousarray(inputs[name])
        arrays[f"in_{name}"] = a
        args.append(nc.dram_tensor(f"in_{name}", a.shape, _mybir.dt.from_np(a.dtype), kind="ExternalInput").ap())
    out = nc.dram_tensor("out_0", (N, D), _mybir.dt.float32, kind="ExternalOutput").ap()
    build(nc, *args, out)
    r = _run(nc, [arrays], core_ids=[0])
    return r.results[0]["out_0"]
```
